# Optimizing a Trainium2 kernel written in Bass

```python
import numpy as np
import jax
import jax.numpy as jnp

def _softmax(x, axis=-1):
    return jax.nn.softmax(x, axis=axis)

def _gelu(x):
    return jax.nn.gelu(x, approximate=True)

def _silu(x):
    return jax.nn.silu(x)

def _sigmoid(x):
    return jax.nn.sigmoid(x)

def _layernorm(x, axis=-1, eps=1e-05):
    m = jnp.mean(x, axis=axis, keepdims=True)
    v = jnp.var(x, axis=axis, keepdims=True)
    return (x - m) / jnp.sqrt(v + eps)

def _scatter_add(tgt, idx, src, axis=0):
    return tgt.at[idx].add(src)

def _segment_sum(src, seg, n):
    return jax.ops.segment_sum(src, seg, n)
kernel_name = 'mk_perceiver_d1_seqx_r2_c8b27d'

def setup_inputs(seed: int=0):
    np.random.seed(seed)
    _w = jnp.asarray

    def _rec_inputs():
        import jax
        import jax.numpy as jnp
        _rk = jax.random.key(seed)
        x = 7.22e-05 + 1 * jax.random.normal(jax.random.fold_in(_rk, 1), (1, 512, 512), jnp.float32)
        _lenS = 512 - jax.random.randint(jax.random.fold_in(_rk, 7), (1,), 0, max(1, 512 // 4) + 1, jnp.int32)
        _lenS2 = 8192 - jax.random.randint(jax.random.fold_in(_rk, 8), (1,), 0, max(1, 8192 // 4) + 1, jnp.int32)
        _ctx_1024P = jax.random.normal(jax.random.fold_in(_rk, 11), (1, 16, 512), jnp.float32)
        _ctx_1024c = jax.random.dirichlet(jax.random.fold_in(_rk, 511), 0.3 * jnp.ones((16,), jnp.float32), (1, 8192))
        _ctx_1024t = jnp.einsum('bsk,bkd->bsd', _ctx_1024c, _ctx_1024P)
        _ctx_1024t = _ctx_1024t * jax.lax.rsqrt(jnp.mean(jnp.square(_ctx_1024t)) + 1e-12) * 0.953939
        ctx_1024 = 4.13588e-05 + 0.999923 * (_ctx_1024t + 0.3 * jax.random.normal(jax.random.fold_in(_rk, 611), (1, 8192, 512), jnp.float32))
        fside_BxSxS2_0 = -1.47943e-05 + 1.00017 * jax.random.normal(jax.random.fold_in(_rk, 12), (1, 512, 8192), jnp.float32)
        return (x, ctx_1024, fside_BxSxS2_0)
    x, ctx_1024, fside_BxSxS2_0 = _rec_inputs()

    def _L0_xattn_setup():
        import jax, jax.numpy as jnp
        import numpy as np
        D = 512
        key = jax.random.key(seed)
        ks = jax.random.split(key, 13)
        B, S, d = (4, 1024, D)
        inp = {'q_in': jax.random.normal(ks[0], (B, S, d), jnp.float32), 'k_in': jax.random.normal(ks[1], (B, S, d), jnp.float32), 'v_in': jax.random.normal(ks[2], (B, S, d), jnp.float32), 'phi_risk': jax.random.normal(ks[3], (B, S, S), jnp.float32), 'phi_prio': jax.random.normal(ks[4], (B, S, S), jnp.float32), 'phi_impl': jax.random.normal(ks[5], (B, S, S), jnp.float32), 'Wq': jax.random.normal(ks[6], (d, d), jnp.float32) / np.sqrt(d), 'bq': jax.random.normal(ks[7], (d,), jnp.float32) * 0.01, 'Wk': jax.random.normal(ks[8], (d, d), jnp.float32) / np.sqrt(d), 'bk': jax.random.normal(ks[9], (d,), jnp.float32) * 0.01, 'Wv': jax.random.normal(ks[10], (d, d), jnp.float32) / np.sqrt(d), 'bv': jax.random.normal(ks[11], (d,), jnp.float32) * 0.01, 'beta_risk': jnp.float32(0.1), 'beta_prio': jnp.float32(0.1), 'beta_impl': jnp.float32(0.1)}
        return inp
    _L0_xattn_all = _L0_xattn_setup()
    _L0_xattn_in = {k: v for k, v in _L0_xattn_all.items() if k in ('Wq', 'bq', 'Wk', 'bk', 'Wv', 'bv', 'beta_risk', 'beta_prio', 'beta_impl')}
    del _L0_xattn_all

    def _L0_attn_setup():
        import jax, jax.numpy as jnp
        import numpy as np
        import math
        DIM = 512
        ATTN_DIM = 512
        B, S = (2, 2048)
        key = jax.random.key(seed)
        k1, k2, k3 = jax.random.split(key, 3)
        x = jax.random.normal(k1, (B, S, DIM), dtype=jnp.float32)
        W_qkv = jax.random.normal(k2, (3 * ATTN_DIM, DIM), dtype=jnp.float32) * (1.0 / math.sqrt(DIM))
        b_qkv = jax.random.normal(k3, (3 * ATTN_DIM,), dtype=jnp.float32) * 0.01
        return {'x': x, 'W_qkv': W_qkv, 'b_qkv': b_qkv}
    _L0_attn_all = _L0_attn_setup()
    _L0_attn_in = {k: v for k, v in _L0_attn_all.items() if k in ('W_qkv', 'b_qkv')}
    del _L0_attn_all

    def _L0_ffn_setup():
        import jax, jax.numpy as jnp
        import numpy as np
        HIDDEN_SIZE = 512
        NUM_EXPERTS = 8
        MOE_INTERMEDIATE_SIZE = 704
        NUM_EXPERTS_PER_TOK = 2
        SHARED_EXPERT_INTERMEDIATE_SIZE = 1408
        B, T = (2, 512)
        W_SCALE = 0.02
        key = jax.random.key(seed)
        ks = jax.random.split(key, 8)
        H, E, I, SI = (HIDDEN_SIZE, NUM_EXPERTS, MOE_INTERMEDIATE_SIZE, SHARED_EXPERT_INTERMEDIATE_SIZE)
        return {'x': jax.random.normal(ks[0], (B, T, H), jnp.float32), 'gate_w': jax.random.normal(ks[1], (E, H), jnp.float32) * W_SCALE, 'experts_gate_up': jax.random.normal(ks[2], (E, 2 * I, H), jnp.float32) * W_SCALE, 'experts_down': jax.random.normal(ks[3], (E, H, I), jnp.float32) * W_SCALE, 'shared_gate_w': jax.random.normal(ks[4], (SI, H), jnp.float32) * W_SCALE, 'shared_up_w': jax.random.normal(ks[5], (SI, H), jnp.float32) * W_SCALE, 'shared_down_w': jax.random.normal(ks[6], (H, SI), jnp.float32) * W_SCALE, 'shared_expert_gate_w': jax.random.normal(ks[7], (1, H), jnp.float32) * W_SCALE}
    _L0_ffn_all = _L0_ffn_setup()
    _L0_ffn_in = {k: v for k, v in _L0_ffn_all.items() if k in ('gate_w', 'experts_gate_up', 'experts_down', 'shared_gate_w', 'shared_up_w', 'shared_down_w', 'shared_expert_gate_w')}
    del _L0_ffn_all
    return {'x': x, 'ctx_1024': ctx_1024, 'fside_BxSxS2_0': fside_BxSxS2_0, 'L0_xattn_Wq': _L0_xattn_in['Wq'], 'L0_xattn_bq': _L0_xattn_in['bq'], 'L0_xattn_Wk': _L0_xattn_in['Wk'], 'L0_xattn_bk': _L0_xattn_in['bk'], 'L0_xattn_Wv': _L0_xattn_in['Wv'], 'L0_xattn_bv': _L0_xattn_in['bv'], 'L0_xattn_beta_risk': _L0_xattn_in['beta_risk'], 'L0_xattn_beta_prio': _L0_xattn_in['beta_prio'], 'L0_xattn_beta_impl': _L0_xattn_in['beta_impl'], 'L0_attn_W_qkv': _L0_attn_in['W_qkv'], 'L0_attn_b_qkv': _L0_attn_in['b_qkv'], 'L0_ffn_gate_w': _L0_ffn_in['gate_w'], 'L0_ffn_experts_gate_up': _L0_ffn_in['experts_gate_up'], 'L0_ffn_experts_down': _L0_ffn_in['experts_down'], 'L0_ffn_shared_gate_w': _L0_ffn_in['shared_gate_w'], 'L0_ffn_shared_up_w': _L0_ffn_in['shared_up_w'], 'L0_ffn_shared_down_w': _L0_ffn_in['shared_down_w'], 'L0_ffn_shared_expert_gate_w': _L0_ffn_in['shared_expert_gate_w']}

def reference(x, ctx_1024, fside_BxSxS2_0, L0_xattn_Wq, L0_xattn_bq, L0_xattn_Wk, L0_xattn_bk, L0_xattn_Wv, L0_xattn_bv, L0_xattn_beta_risk, L0_xattn_beta_prio, L0_xattn_beta_impl, L0_attn_W_qkv, L0_attn_b_qkv, L0_ffn_gate_w, L0_ffn_experts_gate_up, L0_ffn_experts_down, L0_ffn_shared_gate_w, L0_ffn_shared_up_w, L0_ffn_shared_down_w, L0_ffn_shared_expert_gate_w):
    import jax
    import jax.numpy as jnp

    def _L0_xattn_ref(q_in, k_in, v_in, phi_risk, phi_prio, phi_impl, Wq, bq, Wk, bk, Wv, bv, beta_risk, beta_prio, beta_impl):
        import jax, jax.numpy as jnp
        import numpy as np
        D = 512
        d = q_in.shape[-1]
        scale = jnp.asarray(d, q_in.dtype) ** (-0.5)
        Q = q_in @ Wq.T + bq
        K = k_in @ Wk.T + bk
        V = v_in @ Wv.T + bv
        att = jnp.einsum('bsd,btd->bst', Q, K) * scale
        att = att + beta_risk * phi_risk + beta_prio * phi_prio - beta_impl * phi_impl
        w = jax.nn.softmax(att, axis=-1)
        return jnp.einsum('bst,btd->bsd', w, V)

    def _L0_attn_ref(x, W_qkv, b_qkv):
        import jax, jax.numpy as jnp
        import numpy as np
        import math
        DIM = 512
        ATTN_DIM = 512
        B, S = (2, 2048)
        b, s, d = x.shape
        qkv = jnp.einsum('bsd,ed->bse', x, W_qkv) + b_qkv
        q, k, v = jnp.split(qkv, 3, axis=-1)
        score = jnp.einsum('bqd,bkd->bqk', q, k)
        causal = jnp.tril(jnp.ones((s, s), dtype=bool))
        score = jnp.where(causal, score, -jnp.inf)
        attn = jax.nn.softmax(score / math.sqrt(ATTN_DIM), axis=-1)
        y = jnp.einsum('bqk,bkd->bqd', attn, v)
        return y

    def _L0_ffn_ref(x, gate_w, experts_gate_up, experts_down, shared_gate_w, shared_up_w, shared_down_w, shared_expert_gate_w):
        import jax, jax.numpy as jnp
        import numpy as np
        HIDDEN_SIZE = 512
        NUM_EXPERTS = 8
        MOE_INTERMEDIATE_SIZE = 704
        NUM_EXPERTS_PER_TOK = 2
        SHARED_EXPERT_INTERMEDIATE_SIZE = 1408
        B, T = (2, 512)
        W_SCALE = 0.02
        Bx, Tx, H = x.shape
        E = gate_w.shape[0]
        I = experts_down.shape[2]
        x_flat = x.reshape(Bx * Tx, H)
        logits = x_flat @ gate_w.T
        scores = jax.nn.softmax(logits, axis=-1)
        _, topk_ids = jax.lax.top_k(scores, NUM_EXPERTS_PER_TOK)
        in_topk = jax.nn.one_hot(topk_ids, E, dtype=x.dtype).sum(axis=1)
        w = scores * in_topk
        gu = jnp.einsum('nh,eih->nei', x_flat, experts_gate_up)
        g, u = (gu[..., :I], gu[..., I:])
        h = jax.nn.silu(g) * u
        expert_out = jnp.einsum('nei,ehi->neh', h, experts_down)
        out = jnp.einsum('neh,ne->nh', expert_out, w)
        shared = jax.nn.silu(x_flat @ shared_gate_w.T) * (x_flat @ shared_up_w.T) @ shared_down_w.T
        shared_weight = jax.nn.sigmoid(x_flat @ shared_expert_gate_w.T)
        out = out + shared_weight * shared
        return out.reshape(Bx, Tx, H)
    x = x + _L0_xattn_ref(_layernorm(x, axis=-1), ctx_1024, ctx_1024, fside_BxSxS2_0, fside_BxSxS2_0, fside_BxSxS2_0, L0_xattn_Wq, L0_xattn_bq, L0_xattn_Wk, L0_xattn_bk, L0_xattn_Wv, L0_xattn_bv, L0_xattn_beta_risk, L0_xattn_beta_prio, L0_xattn_beta_impl)
    x = x + _L0_attn_ref(_layernorm(x, axis=-1), L0_attn_W_qkv, L0_attn_b_qkv)
    x = x + _L0_ffn_ref(_layernorm(x, axis=-1), L0_ffn_gate_w, L0_ffn_experts_gate_up, L0_ffn_experts_down, L0_ffn_shared_gate_w, L0_ffn_shared_up_w, L0_ffn_shared_down_w, L0_ffn_shared_expert_gate_w)
    return x

_drawn_inputs = setup_inputs


def setup_inputs(seed=0):
    import zlib

    import numpy as np

    out = dict(_drawn_inputs(seed))
    spreads = {}
    factors = {'fside_BxSxS2_0': 8.0,
     'L0_xattn_bq': 8.0,
     'L0_xattn_bk': 64.0,
     'L0_xattn_bv': 5.258,
     'L0_attn_b_qkv': 7.116,
     'L0_ffn_gate_w': 4.688,
     'L0_ffn_experts_gate_up': 3.941,
     'L0_ffn_experts_down': 3.93,
     'L0_ffn_shared_expert_gate_w': 55.206,
     'L0_ffn_shared_gate_w': 3.16,
     'L0_ffn_shared_up_w': 3.115,
     'L0_ffn_shared_down_w': 3.096}
    for name, (base, spread) in spreads.items():
        noise = np.random.default_rng([zlib.crc32(name.encode()), seed]).standard_normal(out[name].shape)
        drawn = base * np.exp(spread * noise) if base else spread * noise
        out[name] = jnp.asarray(drawn.astype(out[name].dtype))
    for name, factor in factors.items():
        out[name] = (out[name] * factor).astype(out[name].dtype)
    return out
```

```python
from contextlib import ExitStack

import concourse.bass as bass
from concourse import mybir

F32 = mybir.dt.float32
F32R = mybir.dt.float32r
ALU = mybir.AluOpType
ACT = mybir.ActivationFunctionType
AX_X = mybir.AxisListType.X

P = 128
D = 512
S = 512
T = 8192
KC = D // P
ST = S // P
CT = T // P
U = 4
E = 8
NI = 704
GROUPS = E // 2 + 1
GT = 2 * NI // P
MIX = NI // P
WB = 3 * (E // 2) + 1
EPS = 1e-5
SCALE = float(D) ** -0.5
NEG = -1.0e30
WB_BANKS = (4, 6, 7)
HL = 3
SB = 4
CREDIT = 3


def perceiver_layer(nc, x_in, stream1, ctx_in, wq_in, wk_in, wv_in, wqkv_in, gate_in, ffn_in,
                    cols_in, bv_in, bqkv_in, betas_in, out):
    with ExitStack() as scope:
        KB = 1024
        base = 16512

        def at(name, shape, dt, kb):
            return nc.alloc_sbuf_tensor_at(name, shape, dt, offset=base + int(kb * KB))

        def sem(name):
            return scope.enter_context(nc.semaphore(name))

        x = at("x", [P, ST, D], F32, 0)
        ident = at("ident", [P, P], F32, 8)
        ones = at("ones", [P, P], F32, 8.5)
        causal = at("causal", [P, P], F32, 9)
        lower = at("lower", [P, E * E], F32, 9.5)
        gate = at("gate", [P, KC, E + 1], F32, 9.75)
        cols = at("cols", [P, 20], F32, 10)
        stats = at("stats", [P, ST, 6], F32, 10.125)
        mv = at("mv", [P, ST, 2], F32, 10.25)
        std = at("std", [P, ST], F32, 10.3125)
        rstd = at("rstd", [P, ST], F32, 10.34375)
        beta = at("beta", [P, 1], F32, 10.375)
        mcol = at("mcol", [P, ST], F32, 10.40625)
        nbias = at("nbias", [P, ST], F32, 10.4375)
        rowsum = at("rowsum", [P, ST], F32, 10.46875)
        rinv = at("rinv", [P, ST], F32, 10.5)
        betas = at("betas", [P, 3], F32, 10.53125)
        lg = at("lg", [P, ST, E + 1], F32, 10.5625)
        ex = at("ex", [P, ST, E + 1], F32, 10.75)
        wn = at("wn", [P, ST, E + 1], F32, 11)
        rank = at("rank", [P, ST, E], F32, 11.25)
        qk_hi = at("qk_hi", [P, KC, S], F32R, 12)
        qk_lo = at("qk_lo", [P, KC, S], F32R, 20)
        runmax = at("runmax", [P, S], F32, 28)
        shift = at("shift", [P, S], F32, 30)
        ring1 = at("ring1", [P, U, 2, D], F32, 32)
        ring2 = at("ring2", [P, U, D], F32, 48)
        c_hi = at("c_hi", [P, 2, D], F32R, 56)
        c_lo = at("c_lo", [P, 2, D], F32R, 60)
        p32 = at("p32", [P, 2, S], F32, 64)
        p_hi = at("p_hi", [P, 2, S], F32R, 68)
        p_lo = at("p_lo", [P, 2, S], F32R, 72)
        att = at("att", [P, CT, S], F32, 76)
        expsum = at("expsum", [P, S], F32, 204)
        qb = at("qb", [P, S], F32, 204)
        zero16 = at("zero16", [P, P], mybir.dt.bfloat16, 206)
        wq = at("wq", [P, KC, D], F32, 116)
        wk = at("wk", [P, KC, D], F32, 124)
        ln_a = at("ln_a", [P, ST, D], F32, 132)
        lnT_a = at("lnT_a", [P, KC, S], F32, 140)
        qT_a = at("qT_a", [P, KC, S], F32, 148)
        qk32 = at("qk32", [P, KC, S], F32, 156)
        bkb = at("bkb", [P, KC, P], F32, 164)
        shift_t = at("shift_t", [P, S], F32, 32)
        diag = at("diag", [P, ST, P], F32, 34)
        bv_b = at("bv_b", [P, D], F32, 170)
        wv = at("wv", [P, KC, D], F32, 76)
        wqkv = at("wqkv", [P, KC, 3 * D], F32, 84)
        rsum_b = at("rsum_b", [P, S], F32, 28)
        ln = at("ln", [P, ST, D], F32, 174)
        lnT = at("lnT", [P, KC, S], F32, 182)
        cT = at("cT", [P, KC, S], F32, 190)
        qT = at("qT", [P, KC, S], F32, 12)
        kT = at("kT", [P, KC, S], F32, 20)
        v = at("v", [P, ST, D], F32, 32)
        probs = at("probs", [P, ST, S], F32, 40)
        pT = at("pT", [P, ST, S], F32, 48)
        bqkv_b = at("bqkv_b", [P, D], F32, 198)
        raw = at("raw", [P, GT, 3, D], F32, 108)
        w_hi = at("w_hi", [P, HL, 3, D], F32R, 12)
        w_lo = at("w_lo", [P, HL, 3, D], F32R, 30)
        gated = at("gated", [P, 2, S], F32, 48)
        hid32 = at("hid32", [P, 2, S], F32, 52)
        h_hi = at("h_hi", [P, 2, S], F32R, 56)
        h_lo = at("h_lo", [P, 2, S], F32R, 60)
        ln3T = at("ln3T", [P, KC, S], F32, 64)
        l_hi = at("l_hi", [P, KC, S], F32R, 182)
        l_lo = at("l_lo", [P, KC, S], F32R, 190)
        wb = at("wb", [P, WB, S], F32, 76)
        wT = at("wT", [P, S], F32, 102)
        sel = at("sel", [P, WB, P], F32, 198)
        cmp_gt = at("cmp_gt", [P, ST, E * E], F32, 72)
        cmp_ge = at("cmp_ge", [P, ST, E * E], F32, 73)

        ps = scope.enter_context(nc.psum_tensor("ps", [P, 8, 512], F32))

        x_loaded, wqk_loaded, small_loaded = sem("x_loaded"), sem("wqk_loaded"), sem("small_loaded")
        wv_loaded, wqkv_loaded, bqkv_loaded, out_stored = sem("wv_loaded"), sem("wqkv_loaded"), sem("bqkv_loaded"), sem("out_stored")
        ring1_full = [sem(f"ring1_full{s}") for s in range(U)]
        ring2_full = [sem(f"ring2_full{s}") for s in range(U)]
        raw_full = [sem(f"raw_full{s}") for s in range(GT)]
        pool_step, dve_step = sem("pool_step"), sem("dve_step")
        consts_ready = sem("consts_ready")
        var_ready, std_ready, ln_ready = sem("var_ready"), sem("std_ready"), sem("ln_ready")
        lnT_psum, lnT_ready = sem("lnT_psum"), sem("lnT_ready")
        q_psum, q_ready, qk_psum, qk_ready = sem("q_psum"), sem("q_ready"), sem("qk_psum"), sem("qk_ready")
        bkb_ready, qb_psum = sem("bkb_ready"), sem("qb_psum")
        hi1_ready, lo1_ready, s_psum = sem("hi1_ready"), sem("lo1_ready"), sem("s_psum")
        att_ready, max_done = sem("att_ready"), sem("max_done")
        maxT_psum, diag_ready, maxb_psum, shift_ready = sem("maxT_psum"), sem("diag_ready"), sem("maxb_psum"), sem("shift_ready")
        shifted, exp_done, p_hi_ready, p_lo_ready, summed = sem("shifted"), sem("exp_done"), sem("p_hi_ready"), sem("p_lo_ready"), sem("summed")
        hi2_ready, lo2_ready, pv_done = sem("hi2_ready"), sem("lo2_ready"), sem("pv_done")
        sum_psum, cT_ready, o_psum, x_ready = sem("sum_psum"), sem("cT_ready"), sem("o_psum"), sem("x_ready")
        qkv_psum, qk2_ready, v_ready = sem("qkv_psum"), sem("qk2_ready"), sem("v_ready")
        sc_psum, nbias_ready, probs_ready, pT_psum, pT_ready, y_psum = sem("sc_psum"), sem("nbias_ready"), sem("probs_ready"), sem("pT_psum"), sem("pT_ready"), sem("y_psum")
        split3_ready, logit_psum, logit_ready, gexp_ready, wn_ready = sem("split3_ready"), sem("logit_psum"), sem("logit_ready"), sem("gexp_ready"), sem("wn_ready")
        wT_psum, wT_ready, wb_psum, wb_even, wb_odd = sem("wT_psum"), sem("wT_ready"), sem("wb_psum"), sem("wb_even"), sem("wb_odd")
        whi_ready, wlo_ready, g_psum, u_psum = sem("whi_ready"), sem("wlo_ready"), sem("g_psum"), sem("u_psum")
        silu_done, prod_done, hid_done, hhi_ready, h_ready, down_done = sem("silu_done"), sem("prod_done"), sem("hid_done"), sem("hhi_ready"), sem("h_ready"), sem("down_done")
        y_ready = sem("y_ready")

        def split_reuse(j):
            return 2 if j < 2 else 5 if j == 2 else HL

        def pair_reuse(j):
            return 1 if j == 0 else 3 if j == 1 else 2

        block = scope.enter_context(nc.Block())

        @block.sync
        def _(sp):
            sp.dma_start(x[:, :, :], x_in.rearrange("(t p) d -> p t d", p=P)).then_inc(x_loaded, 16)
            sp.dma_start(wq[:, :, :], wq_in).then_inc(wqk_loaded, 16)
            sp.dma_start(wk[:, :, :], wk_in).then_inc(wqk_loaded, 16)
            for s in range(U):
                sp.dma_start(ring1[:, s, :, :], stream1[s]).then_inc(ring1_full[s], 16)
            with sp.Fori(1, CT // U) as g:
                for s in range(U):
                    sp.wait_ge(att_ready, g * U + (s - U + 1 + SB))
                    sp.dma_start(ring1[:, s, :, :], stream1[g * U + s]).then_inc(ring1_full[s], 16)
            for s in range(U):
                sp.dma_start(ring2[:, s, :], ctx_in[s]).then_inc(ring2_full[s], 16)
            with sp.Fori(1, CT // U) as g:
                for s in range(U):
                    sp.wait_ge(lo2_ready, g * U + (s - U + 1))
                    sp.dma_start(ring2[:, s, :], ctx_in[g * U + s]).then_inc(ring2_full[s], 16)
            sp.wait_ge(exp_done, 16)
            sp.dma_start(wv[:, :, :], wv_in).then_inc(wv_loaded, 16)
            sp.dma_start(wqkv[:, :, :], wqkv_in).then_inc(wqkv_loaded, 16)
            for j in range(GT):
                sp.wait_ge(exp_done, 19 + 3 * j)
                sp.dma_start(raw[:, j, :, :], ffn_in[j]).then_inc(raw_full[j], 16)
            with sp.Fori(1, GROUPS) as g:
                for j in range(GT):
                    sp.wait_ge(wlo_ready, g * GT + (j - GT + 1))
                    sp.dma_start(raw[:, j, :, :], ffn_in[g * GT + j]).then_inc(raw_full[j], 16)
            for st in range(ST):
                sp.wait_ge(y_ready, st + 1)
                sp.dma_start(out[st * P:(st + 1) * P, :], x[:, st, :]).then_inc(out_stored, 16)
            sp.wait_ge(out_stored, 16 * ST)

        @block.gpsimd
        def _(pool):
            steps = [0]

            def step(ins):
                steps[0] += 1
                ins.then_inc(pool_step, 1)
                pool.wait_ge(pool_step, steps[0])

            step(pool.memset(ident[:, :], 0.0))
            step(pool.affine_select(out=ident[:, :], in_=ident[:, :], compare_op=ALU.not_equal, fill=1.0,
                                    base=0, pattern=[[-1, P]], channel_multiplier=1))
            step(pool.memset(ones[:, :], 1.0))
            step(pool.memset(causal[:, :], 0.0))
            step(pool.affine_select(out=causal[:, :], in_=causal[:, :], compare_op=ALU.is_ge, fill=NEG,
                                    base=0, pattern=[[-1, P]], channel_multiplier=1))
            step(pool.memset(lower[:, :], 1.0))
            low = lower[:, :].rearrange("p (e j) -> p e j", j=E)
            pool.affine_select(out=low, in_=low, compare_op=ALU.is_gt, fill=0.0,
                               base=0, pattern=[[1, E], [-1, E]], channel_multiplier=0).then_inc(consts_ready, 1)

            with pool.Fori(0, CT // U) as g:
                for s in range(U):
                    pool.wait_ge(hi1_ready, g * U + (s + 1))
                    pool.tensor_tensor(c_lo[:, s % 2, :], ring1[:, s, 0, :], c_hi[:, s % 2, :].bitcast(F32),
                                       ALU.subtract).then_inc(lo1_ready, 1)
            pool.wait_ge(shift_ready, 1)
            with pool.Fori(0, CT // U) as g:
                rows = att[:, bass.ds(g * U, U), :]
                pool.tensor_tensor(rows, rows, shift[:, :].unsqueeze(1).to_broadcast([P, U, S]),
                                   ALU.add).then_inc(shifted, 1)
            with pool.Fori(0, GROUPS) as g:
                for j in range(GT):
                    pool.wait_ge(whi_ready, g * GT + (j + 1))
                    pool.tensor_tensor(w_lo[:, j % HL, :, :], raw[:, j, :, :], w_hi[:, j % HL, :, :].bitcast(F32),
                                       ALU.subtract).then_inc(wlo_ready, 1)

        @block.scalar
        def _(act):
            act.dma_start(cols[:, 0:16], cols_in).then_inc(small_loaded, 16)
            act.dma_start(betas[:, :], betas_in.to_broadcast([P, 3])).then_inc(small_loaded, 16)
            act.dma_start(gate[:, :, :], gate_in).then_inc(small_loaded, 16)
            act.dma_start(bv_b[:, :], bv_in.to_broadcast([P, D])).then_inc(small_loaded, 16)

            def root(n):
                act.wait_ge(var_ready, n)
                act.activation(std[:, :], mv[:, :, 1], ACT.Sqrt).then_inc(std_ready, 1)

            def evacuate_lnT(n, to, bank):
                for k in range(KC):
                    act.wait_ge(lnT_psum, (n - 1) * KC + k + 1)
                    act.activation(to[:, k, :], ps[:, bank + k, :], ACT.Copy).then_inc(lnT_ready, 1)

            root(1)
            evacuate_lnT(1, lnT_a, 4)
            act.wait_ge(small_loaded, 64)
            for e in range(KC):
                act.wait_ge(q_psum, e + 1)
                act.activation(qT_a[:, e, :], ps[:, e, :], ACT.Identity, bias=cols[:, e:e + 1]).then_inc(q_ready, 1)
            with act.Fori(0, CT // U) as g:
                for s in range(U):
                    act.wait_ge(s_psum, g * U + (s + 1))
                    act.wait_ge(ring1_full[s], g * 16 + 16)
                    act.activation(c_hi[:, s % 2, :], ring1[:, s, 0, :], ACT.Copy).then_inc(hi1_ready, 1)
            act.wait_ge(s_psum, CT + 2)
            with act.Fori(0, CT // U) as g:
                for s in range(U):
                    act.wait_ge(pv_done, g * U + (s + 1))
                    act.wait_ge(ring2_full[s], g * 16 + 16)
                    act.activation(c_hi[:, s % 2, :], ring2[:, s, :], ACT.Copy).then_inc(hi2_ready, 1)
                    if s == 0:
                        act.wait_ge(shifted, g + 1)
                    act.wait_ge(summed, g * U + (s + 1))
                    act.activation(p32[:, s % 2, :], att[:, g * U + s, :], ACT.Exp).then_inc(exp_done, 1)
                    act.wait_ge(exp_done, g * U + (s + 1))
                    act.activation(p_hi[:, s % 2, :], p32[:, s % 2, :], ACT.Copy).then_inc(p_hi_ready, 1)

            act.wait_ge(sum_psum, 1)
            act.dma_start(bqkv_b[:, :], bqkv_in.to_broadcast([P, D])).then_inc(bqkv_loaded, 16)
            root(2)
            evacuate_lnT(2, lnT, 4)
            for j in range(2 * KC):
                act.wait_ge(qkv_psum, j + 1)
                to = (qT if j < KC else kT)[:, j % KC, :]
                act.activation(to, ps[:, j, :], ACT.Identity, bias=cols[:, 8 + j:9 + j]).then_inc(qk2_ready, 1)
            for i in range(ST):
                w = (i + 1) * P
                act.wait_ge(nbias_ready, i + 1)
                act.activation(probs[:, i, 0:w], ps[:, 4 + i, 0:w], ACT.Exp, bias=nbias[:, i:i + 1], scale=SCALE,
                               accum_out=rowsum[:, i:i + 1]).then_inc(probs_ready, 1)
                act.wait_ge(pT_psum, i + 1)
                act.activation(pT[:, i, 0:w], ps[:, i, 0:w], ACT.Copy).then_inc(pT_ready, 1)

            def high_parts(g, j):
                act.wait_ge(down_done, g * GT + (j - split_reuse(j) + 1 + CREDIT))
                act.wait_ge(raw_full[j], g * 16 + 16)
                act.activation(w_hi[:, j % HL, :, :], raw[:, j, :, :], ACT.Copy).then_inc(whi_ready, 1)

            def silu(g, j):
                act.wait_ge(g_psum, g * GT + (j + 1))
                act.wait_ge(prod_done, g * GT + (j - pair_reuse(j) + 1 + CREDIT))
                act.activation(gated[:, j % 2, :], ps[:, j % 2, :], ACT.Silu).then_inc(silu_done, 1)

            def group(g, last):
                for j in range(GT):
                    if j + 1 < GT:
                        high_parts(g, j + 1)
                    elif not last:
                        high_parts(g + 1, 0)
                    silu(g, j)

            root(3)
            act.wait_ge(y_psum, ST)
            high_parts(0, 0)
            evacuate_lnT(3, ln3T, 0)
            act.wait_ge(logit_ready, 1)
            act.activation(ex[:, :, 0:E], lg[:, :, 0:E], ACT.Exp).then_inc(gexp_ready, 1)
            act.activation(ex[:, :, E], lg[:, :, E], ACT.Exp, scale=-1.0).then_inc(gexp_ready, 1)
            for m in range(0, WB, 2):
                act.wait_ge(wb_psum, m + 1)
                act.activation(wb[:, m, :], ps[:, WB_BANKS[m % 3], :], ACT.Copy).then_inc(wb_even, 1)
            with act.Fori(0, GROUPS - 1) as g:
                group(g, False)
            group(GROUPS - 1, True)

        @block.tensor
        def _(pe):
            pe.sem_inc(s_psum, 2)
            pe.sem_inc(pv_done, 2)
            pe.sem_inc(down_done, CREDIT)

            def turn_ln(n, src, bank):
                for k in range(KC):
                    for st in range(ST):
                        if k == 0:
                            pe.wait_ge(ln_ready, (n - 1) * ST + st + 1)
                        mm = pe.transpose(ps[:, bank + k, st * P:(st + 1) * P], src[:, st, k * P:(k + 1) * P],
                                          ident[:, :])
                    mm.then_inc(lnT_psum, 1)

            def product(bank, width, lhs, rhs, terms):
                for k in range(terms):
                    mm = pe.matmul(ps[:, bank, 0:width], lhs(k), rhs(k), start=(k == 0), stop=(k == terms - 1))
                return mm

            def open_sums():
                for b in range(4, 8):
                    for q in range(4):
                        pe.matmul(ps[:, b, q * P:(q + 1) * P], zero16[:, :], zero16[:, :], start=(q == 0), stop=False,
                                  skip_group_check=True)

            pe.wait_ge(consts_ready, 1)
            turn_ln(1, ln_a, 4)
            pe.wait_ge(lnT_ready, KC)
            pe.wait_ge(wqk_loaded, 32)
            for e in range(KC):
                product(e, S, lambda k: wq[:, k, e * P:(e + 1) * P], lambda k: lnT_a[:, k, :], KC).then_inc(q_psum, 1)
            pe.wait_ge(q_ready, KC)
            for d in range(KC):
                product(4 + d, S, lambda k: wk[:, k, d * P:(d + 1) * P], lambda k: qT_a[:, k, :], KC).then_inc(qk_psum, 1)
            pe.wait_ge(bkb_ready, 1)
            product(3, S, lambda k: bkb[:, k, :], lambda k: qT_a[:, k, :], KC).then_inc(qb_psum, 1)
            pe.wait_ge(qk_ready, KC + 1)

            with pe.Fori(0, CT // U) as g:
                for s in range(U):
                    pe.wait_ge(hi1_ready, g * U + (s + 1))
                    pe.wait_ge(att_ready, g * U + (s + 1))
                    for k in range(KC):
                        hi = c_hi[:, s % 2, k * P:(k + 1) * P]
                        pe.matmul(ps[:, s, :], hi, qk_hi[:, k, :], start=(k == 0), stop=False)
                        pe.matmul(ps[:, s, :], hi, qk_lo[:, k, :], start=False, stop=False)
                    pe.wait_ge(lo1_ready, g * U + (s + 1))
                    for k in range(KC):
                        mm = pe.matmul(ps[:, s, :], c_lo[:, s % 2, k * P:(k + 1) * P], qk_hi[:, k, :],
                                       start=False, stop=(k == KC - 1))
                    mm.then_inc(s_psum, 1)
            pe.wait_ge(max_done, CT + 1)
            for q in range(ST):
                mm = pe.transpose(ps[:, 0, q * P:(q + 1) * P], runmax[:, q * P:(q + 1) * P], ident[:, :])
            mm.then_inc(maxT_psum, 1)
            pe.wait_ge(diag_ready, 1)
            for q in range(ST):
                mm = pe.matmul(ps[:, 1, q * P:(q + 1) * P], ones[:, :], diag[:, q, :], start=True, stop=True)
            mm.then_inc(maxb_psum, 1)

            open_sums()
            with pe.Fori(0, CT // U) as g:
                for s in range(U):
                    pe.wait_ge(hi2_ready, g * U + (s + 1))
                    pe.wait_ge(p_hi_ready, g * U + (s + 1))
                    for d in range(KC):
                        pe.matmul(ps[:, 4 + d, :], c_hi[:, s % 2, d * P:(d + 1) * P], p_hi[:, s % 2, :],
                                  start=False, stop=False, skip_group_check=True)
                    pe.wait_ge(lo2_ready, g * U + (s + 1))
                    for d in range(KC):
                        pe.matmul(ps[:, 4 + d, :], c_lo[:, s % 2, d * P:(d + 1) * P], p_hi[:, s % 2, :],
                                  start=False, stop=False, skip_group_check=True)
                    pe.wait_ge(p_lo_ready, g * U + (s + 1))
                    for d in range(KC):
                        mm = pe.matmul(ps[:, 4 + d, :], c_hi[:, s % 2, d * P:(d + 1) * P], p_lo[:, s % 2, :],
                                       start=False, stop=False, skip_group_check=True)
                    mm.then_inc(pv_done, 1)
            pe.wait_ge(summed, CT + 2)
            pe.matmul(ps[:, 0, :], ones[:, :], expsum[:, :], start=True, stop=True).then_inc(sum_psum, 1)
            pe.wait_ge(wv_loaded, 16)
            pe.wait_ge(cT_ready, KC)
            for st in range(ST):
                product(st, D, lambda k: cT[:, k, st * P:(st + 1) * P], lambda k: wv[:, k, :], KC).then_inc(o_psum, 1)

            turn_ln(2, ln, 4)
            pe.wait_ge(lnT_ready, 2 * KC)
            pe.wait_ge(wqkv_loaded, 16)
            for j in range(2 * KC):
                product(j, S, lambda k: wqkv[:, k, j * P:(j + 1) * P], lambda k: lnT[:, k, :], KC).then_inc(qkv_psum, 1)
            for st in range(ST):
                pe.wait_ge(qk2_ready, st + 1)
                product(st, D, lambda k: lnT[:, k, st * P:(st + 1) * P], lambda k: wqkv[:, k, 2 * D:3 * D],
                        KC).then_inc(qkv_psum, 1)
            pe.wait_ge(qk2_ready, 2 * KC)
            for i in range(ST):
                w = (i + 1) * P
                product(4 + i, w, lambda k: qT[:, k, i * P:(i + 1) * P], lambda k: kT[:, k, 0:w], KC).then_inc(sc_psum, 1)
            for i in range(ST):
                pe.wait_ge(probs_ready, i + 1)
                pe.wait_ge(v_ready, i + 1)
                for k in range(i + 1):
                    mm = pe.transpose(ps[:, i, k * P:(k + 1) * P], probs[:, i, k * P:(k + 1) * P], ident[:, :])
                mm.then_inc(pT_psum, 1)
                pe.wait_ge(pT_ready, i + 1)
                product(4 + i, D, lambda k: pT[:, i, k * P:(k + 1) * P], lambda k: v[:, k, :], i + 1).then_inc(y_psum, 1)

            turn_ln(3, ln, 0)
            pe.wait_ge(lnT_ready, 3 * KC)
            for st in range(ST):
                for k in range(KC):
                    mm = pe.matmul(ps[:, 4, 16 * st:16 * st + E + 1], ln3T[:, k, st * P:(st + 1) * P], gate[:, k, :],
                                   start=(k == 0), stop=(k == KC - 1))
            mm.then_inc(logit_psum, 1)

            def up(g, j):
                n = g * GT
                pe.wait_ge(whi_ready, n + (j + 1))
                pe.wait_ge(wlo_ready, n + (j + 1))
                pe.wait_ge(prod_done, n + (j - pair_reuse(j) + 1 + CREDIT))
                for part, bank, done in ((0, j % 2, g_psum), (1, 2 + j % 2, u_psum)):
                    for k in range(KC):
                        hi, lo = (w[:, j % HL, part, k * P:(k + 1) * P] for w in (w_hi, w_lo))
                        pe.matmul(ps[:, bank, :], hi, l_hi[:, k, :], start=(k == 0), stop=False)
                        pe.matmul(ps[:, bank, :], hi, l_lo[:, k, :], start=False, stop=False)
                        mm = pe.matmul(ps[:, bank, :], lo, l_hi[:, k, :], start=False, stop=(k == KC - 1))
                    mm.then_inc(done, 1)

            def down(g, j):
                pe.wait_ge(h_ready, g * GT + (j + 1))
                for st in range(ST):
                    hi, lo = (h[:, j % 2, st * P:(st + 1) * P] for h in (h_hi, h_lo))
                    for a, b in ((hi, w_hi), (hi, w_lo), (lo, w_hi)):
                        mm = pe.matmul(ps[:, 4 + st, :], a, b[:, j % HL, 2, :], start=False, stop=False,
                                       skip_group_check=True)
                mm.then_inc(down_done, 1)

            pe.wait_ge(split3_ready, KC)
            up(0, 0)
            pe.wait_ge(wn_ready, 1)
            for st in range(ST):
                mm = pe.matmul(ps[0:E + 1, 5, st * P:(st + 1) * P], wn[:, st, :], ident[:, :], start=True, stop=True)
            mm.then_inc(wT_psum, 1)
            pe.wait_ge(wT_ready, 1)
            for m in range(WB):
                if m >= 3:
                    pe.wait_ge(*((wb_odd, (m - 3) // 2 + 1) if m % 2 == 0 else (wb_even, (m - 3) // 2 + 1)))
                pe.matmul(ps[:, WB_BANKS[m % 3], :], sel[0:E + 1, m, :], wT[0:E + 1, :], start=True,
                          stop=True).then_inc(wb_psum, 1)
            pe.wait_ge(wb_even, (WB + 1) // 2)
            pe.wait_ge(wb_odd, WB // 2)
            open_sums()

            def group(g, last):
                for j in range(GT):
                    if j + 1 < GT:
                        up(g, j + 1)
                    elif not last:
                        up(g + 1, 0)
                    down(g, j)

            with pe.Fori(0, GROUPS - 1) as g:
                group(g, False)
            group(GROUPS - 1, True)

        @block.vector
        def _(dve):
            steps = [0]

            def step(ins):
                steps[0] += 1
                ins.then_inc(dve_step, 1)
                dve.wait_ge(dve_step, steps[0])

            def layernorm(n, to):
                for st in range(ST):
                    ins = dve.bn_stats(stats[:, st, :], x[:, st, :])
                step(ins)
                for st in range(ST):
                    ins = dve.bn_aggr(mv[:, st, :], stats[:, st, :])
                step(ins)
                dve.tensor_scalar(mv[:, :, 1], mv[:, :, 1], EPS, None, ALU.add).then_inc(var_ready, 1)
                dve.wait_ge(std_ready, n)
                step(dve.reciprocal(rstd[:, :], std[:, :]))
                for st in range(ST):
                    dve.tensor_scalar(to[:, st, :], x[:, st, :], mv[:, st, 0:1], rstd[:, st:st + 1],
                                      ALU.subtract, ALU.mult).then_inc(ln_ready, 1)

            dve.sem_inc(att_ready, SB)
            dve.sem_inc(summed, 2)
            dve.sem_inc(prod_done, CREDIT)
            dve.wait_ge(x_loaded, 16)
            layernorm(1, ln_a)
            dve.wait_ge(consts_ready, 1)
            dve.wait_ge(small_loaded, 64)
            for k in range(KC):
                ins = dve.tensor_scalar(bkb[:, k, :], ones[:, :], cols[:, 4 + k:5 + k], None, ALU.mult)
            ins.then_inc(bkb_ready, 1)
            dve.wait_ge(ln_ready, ST)
            for st in range(ST):
                ins = dve.tensor_tensor(x[:, st, :], x[:, st, :], bv_b[:, :], ALU.add)
            step(ins)
            step(dve.tensor_tensor(beta[:, :], betas[:, 0:1], betas[:, 1:2], ALU.add))
            step(dve.tensor_tensor(beta[:, :], beta[:, :], betas[:, 2:3], ALU.subtract))
            dve.memset(zero16[:, :], 0.0)
            dve.memset(runmax[:, :], -3.0e38).then_inc(max_done, 1)
            for d in range(KC):
                dve.wait_ge(qk_psum, d + 1)
                step(dve.tensor_scalar(qk32[:, d, :], ps[:, 4 + d, :], SCALE, None, ALU.mult))
                step(dve.tensor_copy(qk_hi[:, d, :], qk32[:, d, :]))
                dve.tensor_tensor(qk_lo[:, d, :], qk32[:, d, :], qk_hi[:, d, :].bitcast(F32),
                                  ALU.subtract).then_inc(qk_ready, 1)
            dve.wait_ge(qb_psum, 1)
            dve.tensor_scalar(qb[:, :], ps[:, 3, :], SCALE, None, ALU.mult).then_inc(qk_ready, 1)

            with dve.Fori(0, CT // U) as g:
                for s in range(U):
                    dve.wait_ge(s_psum, g * U + (s + 1 + 2))
                    dve.scalar_tensor_tensor(out=att[:, g * U + s, :], in0=ring1[:, s, 1, :], scalar=beta[:, 0:1],
                                             in1=ps[:, s, :], op0=ALU.mult, op1=ALU.add).then_inc(att_ready, 1)
                    dve.wait_ge(att_ready, g * U + (s + 1 + SB))
                    dve.wait_ge(max_done, g * U + (s + 1))
                    dve.tensor_tensor(runmax[:, :], runmax[:, :], att[:, g * U + s, :], ALU.max).then_inc(max_done, 1)
            dve.wait_ge(maxT_psum, 1)
            step(dve.tensor_reduce(mcol[:, :], ps[:, 0, :].rearrange("p (q c) -> p q c", q=ST), AX_X, ALU.max))
            for q in range(ST):
                ins = dve.tensor_scalar(diag[:, q, :], ident[:, :], mcol[:, q:q + 1], None, ALU.mult)
            ins.then_inc(diag_ready, 1)
            dve.wait_ge(maxb_psum, 1)
            step(dve.tensor_tensor(shift_t[:, :], ps[:, 1, :], qb[:, :], ALU.add))
            dve.tensor_tensor(shift[:, :], qb[:, :], shift_t[:, :], ALU.subtract).then_inc(shift_ready, 1)
            dve.wait_ge(shift_ready, 1)
            step(dve.memset(expsum[:, :], 0.0))
            with dve.Fori(0, CT // U) as g:
                for s in range(U):
                    dve.wait_ge(hi2_ready, g * U + (s + 1))
                    dve.tensor_tensor(c_lo[:, s % 2, :], ring2[:, s, :], c_hi[:, s % 2, :].bitcast(F32),
                                      ALU.subtract).then_inc(lo2_ready, 1)
                    dve.wait_ge(p_hi_ready, g * U + (s + 1))
                    dve.tensor_tensor(p_lo[:, s % 2, :], p32[:, s % 2, :], p_hi[:, s % 2, :].bitcast(F32),
                                      ALU.subtract).then_inc(p_lo_ready, 1)
                    dve.wait_ge(summed, g * U + (s + 2))
                    dve.tensor_tensor(expsum[:, :], expsum[:, :], p32[:, s % 2, :], ALU.add).then_inc(summed, 1)
            dve.wait_ge(sum_psum, 1)
            step(dve.reciprocal(rsum_b[:, :], ps[:, 0, :]))
            for k in range(KC):
                dve.tensor_tensor(cT[:, k, :], ps[:, 4 + k, :], rsum_b[:, :], ALU.mult).then_inc(cT_ready, 1)
            for st in range(ST):
                dve.wait_ge(o_psum, st + 1)
                ins = dve.tensor_tensor(x[:, st, :], x[:, st, :], ps[:, st, :], ALU.add)
            step(ins)

            layernorm(2, ln)
            dve.wait_ge(bqkv_loaded, 16)
            for st in range(ST):
                dve.wait_ge(qkv_psum, 2 * KC + st + 1)
                dve.tensor_tensor(v[:, st, :], ps[:, st, :], bqkv_b[:, :], ALU.add).then_inc(v_ready, 1)
            for i in range(ST):
                w = (i + 1) * P
                dve.wait_ge(sc_psum, i + 1)
                step(dve.tensor_tensor(ps[:, 4 + i, i * P:w], ps[:, 4 + i, i * P:w], causal[:, :], ALU.add))
                step(dve.tensor_reduce(mcol[:, i:i + 1], ps[:, 4 + i, 0:w], AX_X, ALU.max))
                dve.tensor_scalar(nbias[:, i:i + 1], mcol[:, i:i + 1], -SCALE, None, ALU.mult).then_inc(nbias_ready, 1)
            for i in range(ST):
                dve.wait_ge(probs_ready, i + 1)
                step(dve.reciprocal(rinv[:, i:i + 1], rowsum[:, i:i + 1]))
                dve.wait_ge(y_psum, i + 1)
                step(dve.scalar_tensor_tensor(out=x[:, i, :], in0=ps[:, 4 + i, :], scalar=rinv[:, i:i + 1],
                                              in1=x[:, i, :], op0=ALU.mult, op1=ALU.add))

            layernorm(3, ln)
            for k in range(KC):
                dve.wait_ge(lnT_ready, 2 * KC + k + 1)
                step(dve.tensor_copy(l_hi[:, k, :], ln3T[:, k, :]))
                dve.tensor_tensor(l_lo[:, k, :], ln3T[:, k, :], l_hi[:, k, :].bitcast(F32),
                                  ALU.subtract).then_inc(split3_ready, 1)
            dve.wait_ge(logit_psum, 1)
            step(dve.tensor_copy(lg[:, :, :], ps[:, 4, 0:16 * ST].rearrange("p (t c) -> p t c", c=16)[:, :, 0:E + 1]))
            le = lg[:, :, 0:E]
            step(dve.tensor_reduce(mcol[:, :], le, AX_X, ALU.max))
            step(dve.tensor_tensor(le, le, mcol[:, :].unsqueeze(2).to_broadcast([P, ST, E]), ALU.subtract))
            dve.sem_inc(logit_ready, 1)
            other = le.unsqueeze(2).to_broadcast([P, ST, E, E])
            own = le.unsqueeze(3).to_broadcast([P, ST, E, E])
            gt = cmp_gt[:, :, :].rearrange("p t (e j) -> p t e j", j=E)
            ge = cmp_ge[:, :, :].rearrange("p t (e j) -> p t e j", j=E)
            dve.tensor_tensor(gt, other, own, ALU.is_gt)
            step(dve.tensor_tensor(ge, other, own, ALU.is_ge))
            step(dve.tensor_tensor(cmp_ge[:, :, :], cmp_ge[:, :, :],
                                   lower[:, :].unsqueeze(1).to_broadcast([P, ST, E * E]), ALU.mult))
            step(dve.tensor_tensor(cmp_gt[:, :, :], cmp_gt[:, :, :], cmp_ge[:, :, :], ALU.max))
            step(dve.tensor_reduce(rank[:, :, :], gt, AX_X, ALU.add))
            dve.wait_ge(gexp_ready, 2)
            step(dve.tensor_reduce(rowsum[:, :], ex[:, :, 0:E], AX_X, ALU.add))
            step(dve.reciprocal(rinv[:, :], rowsum[:, :]))
            dve.tensor_scalar(ex[:, :, E], ex[:, :, E], 1.0, None, ALU.add)
            step(dve.scalar_tensor_tensor(out=wn[:, :, 0:E], in0=rank[:, :, :], scalar=2.0, in1=ex[:, :, 0:E],
                                          op0=ALU.is_lt, op1=ALU.mult))
            dve.reciprocal(wn[:, :, E], ex[:, :, E])
            step(dve.tensor_tensor(wn[:, :, 0:E], wn[:, :, 0:E], rinv[:, :].unsqueeze(2).to_broadcast([P, ST, E]),
                                   ALU.mult))
            dve.sem_inc(wn_ready, 1)
            unit = ident[0:E + 1, 0:E + 1]
            pairs = sel[0:E + 1, 0:WB - 1, :].rearrange("p (g a) c -> p g a c", a=3)
            for par in range(2):
                col = unit[:, par:E:2].unsqueeze(2)
                dve.tensor_copy(pairs[:, :, 2 * par, :], col.to_broadcast([E + 1, E // 2, P]))
                ins = dve.tensor_copy(pairs[:, :, 1, par * 64:par * 64 + 64], col.to_broadcast([E + 1, E // 2, 64]))
            step(dve.tensor_copy(sel[0:E + 1, WB - 1, :], unit[:, E:E + 1].to_broadcast([E + 1, P])))
            dve.wait_ge(wT_psum, 1)
            dve.tensor_copy(wT[0:E + 1, :], ps[0:E + 1, 5, :]).then_inc(wT_ready, 1)
            for m in range(1, WB, 2):
                dve.wait_ge(wb_psum, m + 1)
                dve.tensor_copy(wb[:, m, :], ps[:, WB_BANKS[m % 3], :]).then_inc(wb_odd, 1)
            dve.wait_ge(wb_even, (WB + 1) // 2)
            dve.wait_ge(wb_odd, WB // 2)

            def hidden(g, j, weight):
                n = g * GT
                dve.wait_ge(silu_done, n + (j + 1))
                dve.wait_ge(u_psum, n + (j + 1))
                dve.wait_ge(down_done, n + (j - pair_reuse(j) + 1 + CREDIT))
                dve.tensor_tensor(hid32[:, j % 2, :], gated[:, j % 2, :], ps[:, 2 + j % 2, :],
                                  ALU.mult).then_inc(prod_done, 1)
                dve.wait_ge(prod_done, n + (j + 1 + CREDIT))
                dve.tensor_tensor(hid32[:, j % 2, :], hid32[:, j % 2, :], weight, ALU.mult).then_inc(hid_done, 1)
                dve.wait_ge(hid_done, n + (j + 1))
                dve.tensor_copy(h_hi[:, j % 2, :], hid32[:, j % 2, :]).then_inc(hhi_ready, 1)
                dve.wait_ge(hhi_ready, n + (j + 1))
                dve.tensor_tensor(h_lo[:, j % 2, :], hid32[:, j % 2, :], h_hi[:, j % 2, :].bitcast(F32),
                                  ALU.subtract).then_inc(h_ready, 1)

            with dve.Fori(0, GROUPS - 1) as g:
                for j in range(GT):
                    kind = 0 if j < MIX else 1 if j == MIX else 2
                    hidden(g, j, wb[:, g * 3 + kind, :])
            for j in range(GT):
                hidden(GROUPS - 1, j, wb[:, WB - 1, :])
            dve.wait_ge(down_done, GROUPS * GT + CREDIT)
            for st in range(ST):
                dve.tensor_tensor(x[:, st, :], x[:, st, :], ps[:, 4 + st, :], ALU.add).then_inc(y_ready, 1)


def kernel(x, ctx_1024, fside_BxSxS2_0, L0_xattn_Wq, L0_xattn_bq, L0_xattn_Wk, L0_xattn_bk, L0_xattn_Wv, L0_xattn_bv,
           L0_xattn_beta_risk, L0_xattn_beta_prio, L0_xattn_beta_impl, L0_attn_W_qkv, L0_attn_b_qkv, L0_ffn_gate_w,
           L0_ffn_experts_gate_up, L0_ffn_experts_down, L0_ffn_shared_gate_w, L0_ffn_shared_up_w,
           L0_ffn_shared_down_w, L0_ffn_shared_expert_gate_w):
    import numpy as np
    import concourse.bacc as bacc
    from concourse.bass_utils import run_bass_kernel_spmd

    def rows(w):
        w = np.asarray(w)
        return w.reshape(w.shape[0] // P, P, w.shape[1]).transpose(1, 0, 2)

    def columns(b):
        return np.asarray(b).reshape(-1, P).T

    ctx = np.asarray(ctx_1024)[0].reshape(CT, P, KC, P)
    fside = np.asarray(fside_BxSxS2_0)[0]
    stream1 = np.stack([ctx.transpose(0, 3, 2, 1).reshape(CT, P, D), fside.T.reshape(CT, P, S)], axis=2)

    gu = np.asarray(L0_ffn_experts_gate_up)
    gate_rows = np.concatenate([gu[:, :NI].reshape(-1, D), np.asarray(L0_ffn_shared_gate_w)])
    up_rows = np.concatenate([gu[:, NI:].reshape(-1, D), np.asarray(L0_ffn_shared_up_w)])
    down_rows = np.concatenate([np.asarray(L0_ffn_experts_down).transpose(0, 2, 1).reshape(-1, D),
                                np.asarray(L0_ffn_shared_down_w).T])
    tiles = GROUPS * GT

    def turned(w):
        return w.reshape(tiles, P, KC, P).transpose(0, 3, 2, 1).reshape(tiles, P, D)

    b_qkv = np.asarray(L0_attn_b_qkv)
    given = {
        "x_in": np.asarray(x)[0],
        "stream1": stream1,
        "ctx_in": ctx.reshape(CT, P, D),
        "wq_in": rows(np.asarray(L0_xattn_Wq).T),
        "wk_in": rows(L0_xattn_Wk),
        "wv_in": rows(np.asarray(L0_xattn_Wv).T),
        "wqkv_in": rows(np.asarray(L0_attn_W_qkv).T),
        "gate_in": rows(np.concatenate([np.asarray(L0_ffn_gate_w), np.asarray(L0_ffn_shared_expert_gate_w)]).T),
        "ffn_in": np.stack([turned(gate_rows), turned(up_rows), down_rows.reshape(tiles, P, D)], axis=2),
        "cols_in": np.concatenate([columns(L0_xattn_bq), columns(L0_xattn_bk), columns(b_qkv[:2 * D])], axis=1),
        "bv_in": np.asarray(L0_xattn_bv).reshape(1, D),
        "bqkv_in": b_qkv[2 * D:].reshape(1, D),
        "betas_in": np.stack([np.asarray(L0_xattn_beta_risk), np.asarray(L0_xattn_beta_prio),
                              np.asarray(L0_xattn_beta_impl)]).reshape(1, 3),
    }
    given = {name: np.ascontiguousarray(a) for name, a in given.items()}
    nc = bacc.Bacc("TRN2", target_bir_lowering=False, num_devices=1)
    args = {name: nc.dram_tensor(name, a.shape, mybir.dt.from_np(a.dtype), kind="ExternalInput").ap()
            for name, a in given.items()}
    result = nc.dram_tensor("result", (S, D), F32, kind="ExternalOutput").ap()
    perceiver_layer(nc, out=result, **args)
    r = run_bass_kernel_spmd(nc, [given], core_ids=[0])
    return r.results[0]["result"].reshape(1, S, D)
```

```python
from contextlib import ExitStack

import concourse.bass as bass
from concourse import mybir

F32 = mybir.dt.float32
F32R = mybir.dt.float32r
ALU = mybir.AluOpType
ACT = mybir.ActivationFunctionType
AX_X = mybir.AxisListType.X

P = 128
D = 512
S = 512
T = 8192
KC = D // P
ST = S // P
CT = T // P
U = 4
E = 8
NI = 704
GROUPS = E // 2 + 1
GT = 2 * NI // P
MIX = NI // P
WB = 3 * (E // 2) + 1
EPS = 1e-5
SCALE = float(D) ** -0.5
NEG = -1.0e30
WB_BANKS = (4, 6, 7)
HL = 4
R2 = 4
DOWN = tuple(reversed(range(ST)))
SB = 4
CREDIT = 4


def perceiver_layer(nc, x_in, stream1, ctx_in, wq_in, wk_in, wv_in, wqkv_in, gate_in, ffn_in,
                    cols_in, bv_in, bqkv_in, betas_in, out):
    with ExitStack() as scope:
        KB = 1024
        base = 16512

        def at(name, shape, dt, kb):
            return nc.alloc_sbuf_tensor_at(name, shape, dt, offset=base + int(kb * KB))

        def sem(name):
            return scope.enter_context(nc.semaphore(name))

        x = at("x", [P, ST, D], F32, 0)
        ident = at("ident", [P, P], F32, 8)
        ones = at("ones", [P, P], F32, 8.5)
        causal = at("causal", [P, P], F32, 9)
        lower = at("lower", [P, E * E], F32, 9.5)
        gate = at("gate", [P, KC, E + 1], F32, 9.75)
        cols = at("cols", [P, 20], F32, 10)
        stats = at("stats", [P, ST, 6], F32, 10.125)
        mv = at("mv", [P, ST, 2], F32, 10.25)
        std = at("std", [P, ST], F32, 10.3125)
        rstd = at("rstd", [P, ST], F32, 10.34375)
        beta = at("beta", [P, 1], F32, 10.375)
        mcol = at("mcol", [P, ST], F32, 10.40625)
        nbias = at("nbias", [P, ST], F32, 10.4375)
        rowsum = at("rowsum", [P, ST], F32, 10.46875)
        rinv = at("rinv", [P, ST], F32, 10.5)
        betas = at("betas", [P, 3], F32, 10.53125)
        lg = at("lg", [P, ST, E + 1], F32, 10.5625)
        ex = at("ex", [P, ST, E + 1], F32, 10.75)
        wn = at("wn", [P, ST, E + 1], F32, 11)
        rank = at("rank", [P, ST, E], F32, 11.25)
        qk_hi = at("qk_hi", [P, KC, S], F32R, 12)
        qk_lo = at("qk_lo", [P, KC, S], F32R, 20)
        runmax = at("runmax", [P, S], F32, 28)
        shift = at("shift", [P, S], F32, 30)
        ring1 = at("ring1", [P, U, 2, D], F32, 32)
        ring2 = at("ring2", [P, R2, 2, D], F32, 48)
        c_hi = at("c_hi", [P, 2, D], F32R, 68)
        c_lo = at("c_lo", [P, 2, D], F32R, 72)
        d_hi = at("d_hi", [P, 2, 2, D], F32R, 12)
        d_lo = at("d_lo", [P, 2, 2, D], F32R, 20)
        p32 = at("p32", [P, 2, 2, S], F32, 32)
        p_hi = at("p_hi", [P, 2, 2, S], F32R, 40)
        p_lo = at("p_lo", [P, 2, 2, S], F32R, 64)
        expsum = at("expsum", [P, 2, S], F32, 72)
        att = at("att", [P, CT, S], F32, 76)
        qb = at("qb", [P, S], F32, 204)
        zero16 = at("zero16", [P, P], mybir.dt.bfloat16, 206)
        wq = at("wq", [P, KC, D], F32, 116)
        wk = at("wk", [P, KC, D], F32, 124)
        ln_a = at("ln_a", [P, ST, D], F32, 132)
        lnT_a = at("lnT_a", [P, KC, S], F32, 140)
        wqk = at("wqk", [P, KC, D], F32, 148)
        qk32 = at("qk32", [P, KC, S], F32, 156)
        bkb = at("bkb", [P, KC, P], F32, 164)
        ub = at("ub", [P, KC, P], F32, 166)
        cbias = at("cbias", [P, 2 * KC + 1], F32, 168)
        shift_t = at("shift_t", [P, S], F32, 32)
        diag = at("diag", [P, ST, P], F32, 34)
        bv_b = at("bv_b", [P, D], F32, 170)
        wv = at("wv", [P, KC, D], F32, 76)
        wqkv = at("wqkv", [P, KC, 3 * D], F32, 84)
        ln = at("ln", [P, ST, D], F32, 174)
        lnT = at("lnT", [P, KC, S], F32, 182)
        cT = at("cT", [P, KC, S], F32, 190)
        qT = at("qT", [P, KC, S], F32, 12)
        kT = at("kT", [P, KC, S], F32, 20)
        v = at("v", [P, ST, D], F32, 32)
        probs = at("probs", [P, ST, S], F32, 40)
        pT = at("pT", [P, ST, S], F32, 48)
        bqkv_b = at("bqkv_b", [P, D], F32, 198)
        raw = at("raw", [P, GT, 3, D], F32, 108)
        w_hi = at("w_hi", [P, HL, 3, D], F32R, 12)
        w_lo = at("w_lo", [P, HL, 3, D], F32R, 36)
        h_hi = at("h_hi", [P, 2, S], F32R, 60)
        h_lo = at("h_lo", [P, 2, S], F32R, 64)
        gated = at("gated", [P, 2, S], F32, 68)
        hid32 = at("hid32", [P, 2, S], F32, 72)
        ln3T = at("ln3T", [P, KC, S], F32, 60)
        l_hi = at("l_hi", [P, KC, S], F32R, 182)
        l_lo = at("l_lo", [P, KC, S], F32R, 190)
        wb = at("wb", [P, WB, S], F32, 76)
        wT_hi = at("wT_hi", [P, S], F32R, 102)
        wT_lo = at("wT_lo", [P, S], F32R, 104)
        sel = at("sel", [P, WB, P], F32R, 198)
        cmp_gt = at("cmp_gt", [P, ST, E * E], F32, 72)
        cmp_ge = at("cmp_ge", [P, ST, E * E], F32, 73)

        ps = scope.enter_context(nc.psum_tensor("ps", [P, 8, 512], F32))

        x_loaded, wqk_loaded, small_loaded = sem("x_loaded"), sem("wqk_loaded"), sem("small_loaded")
        wv_loaded, wqkv_loaded, bqkv_loaded, out_stored = sem("wv_loaded"), sem("wqkv_loaded"), sem("bqkv_loaded"), sem("out_stored")
        ring1_full = [sem(f"ring1_full{s}") for s in range(U)]
        ring2_full = [sem(f"ring2_full{s}") for s in range(R2)]
        raw_full = [sem(f"raw_full{s}") for s in range(GT)]
        pool_step, dve_step = sem("pool_step"), sem("dve_step")
        consts_ready = sem("consts_ready")
        var_ready, std_ready, ln_ready = sem("var_ready"), sem("std_ready"), sem("ln_ready")
        lnT_psum, lnT_ready = sem("lnT_psum"), sem("lnT_ready")
        wqk_psum, wqk_ready, qk_psum, qk_ready = sem("wqk_psum"), sem("wqk_ready"), sem("qk_psum"), sem("qk_ready")
        bkb_ready, bias_psum, ub_ready, qb_psum = sem("bkb_ready"), sem("bias_psum"), sem("ub_ready"), sem("qb_psum")
        hi1_ready, lo1_ready, s_psum = sem("hi1_ready"), sem("lo1_ready"), sem("s_psum")
        att_ready, max_done = sem("att_ready"), sem("max_done")
        maxT_psum, diag_ready, maxb_psum, shift_ready = sem("maxT_psum"), sem("diag_ready"), sem("maxb_psum"), sem("shift_ready")
        shifted, exp_done, p_hi_ready, p_lo_ready, summed = sem("shifted"), sem("exp_done"), sem("p_hi_ready"), sem("p_lo_ready"), sem("summed")
        hi2_ready, lo2_ready, pv_done = sem("hi2_ready"), sem("lo2_ready"), sem("pv_done")
        sum_psum, cT_even, cT_odd, o_psum = sem("sum_psum"), sem("cT_even"), sem("cT_odd"), sem("o_psum")
        sum_read = sem("sum_read")
        qkv_psum, qk2_ready, v_ready = sem("qkv_psum"), sem("qk2_ready"), sem("v_ready")
        sc_psum, nbias_ready, probs_ready, pT_psum, pT_ready, y_psum = sem("sc_psum"), sem("nbias_ready"), sem("probs_ready"), sem("pT_psum"), sem("pT_ready"), sem("y_psum")
        split3_ready, logit_psum, logit_ready, gexp_ready, wn_ready = sem("split3_ready"), sem("logit_psum"), sem("logit_ready"), sem("gexp_ready"), sem("wn_ready")
        wT_psum, wT_ready, wb_psum, wb_even, wb_odd = sem("wT_psum"), sem("wT_ready"), sem("wb_psum"), sem("wb_even"), sem("wb_odd")
        whi_ready, wlo_ready, g_psum, u_psum = sem("whi_ready"), sem("wlo_ready"), sem("g_psum"), sem("u_psum")
        silu_done, prod_done, hid_done, hhi_ready, h_ready, down_done = sem("silu_done"), sem("prod_done"), sem("hid_done"), sem("hhi_ready"), sem("h_ready"), sem("down_done")
        y_ready = sem("y_ready")

        def split_reuse(j):
            return 3 if j < 3 else 7 if j == 3 else HL

        def pair_reuse(j):
            return 1 if j == 0 else 3 if j == 1 else 2

        block = scope.enter_context(nc.Block())

        @block.sync
        def _(sp):
            sp.dma_start(x[:, :, :], x_in.rearrange("(t p) d -> p t d", p=P)).then_inc(x_loaded, 16)
            sp.dma_start(wq[:, :, :], wq_in).then_inc(wqk_loaded, 16)
            sp.dma_start(wk[:, :, :], wk_in).then_inc(wqk_loaded, 16)
            for s in range(U):
                sp.dma_start(ring1[:, s, :, :], stream1[s]).then_inc(ring1_full[s], 16)
            with sp.Fori(1, CT // U) as g:
                for s in range(U):
                    sp.wait_ge(att_ready, g * U + (s - U + 1 + SB))
                    sp.dma_start(ring1[:, s, :, :], stream1[g * U + s]).then_inc(ring1_full[s], 16)
            for s in range(R2):
                sp.dma_start(ring2[:, s, :, :], ctx_in[s]).then_inc(ring2_full[s], 16)
            with sp.Fori(1, CT // 2 // R2) as g:
                for s in range(R2):
                    sp.wait_ge(lo2_ready, g * R2 + (s - R2 + 1))
                    sp.dma_start(ring2[:, s, :, :], ctx_in[g * R2 + s]).then_inc(ring2_full[s], 16)
            sp.wait_ge(exp_done, 8)
            sp.dma_start(wv[:, :, :], wv_in).then_inc(wv_loaded, 16)
            sp.dma_start(wqkv[:, :, :], wqkv_in).then_inc(wqkv_loaded, 16)
            for j in range(GT):
                sp.wait_ge(exp_done, (19 + 3 * j + 1) // 2)
                sp.dma_start(raw[:, j, :, :], ffn_in[j]).then_inc(raw_full[j], 16)
            with sp.Fori(1, GROUPS) as g:
                for j in range(GT):
                    sp.wait_ge(wlo_ready, g * GT + (j - GT + 1))
                    sp.dma_start(raw[:, j, :, :], ffn_in[g * GT + j]).then_inc(raw_full[j], 16)
            for st in range(ST):
                sp.wait_ge(y_ready, st + 1)
                sp.dma_start(out[st * P:(st + 1) * P, :], x[:, st, :]).then_inc(out_stored, 16)
            sp.wait_ge(out_stored, 16 * ST)

        @block.gpsimd
        def _(pool):
            steps = [0]

            def step(ins):
                steps[0] += 1
                ins.then_inc(pool_step, 1)
                pool.wait_ge(pool_step, steps[0])

            step(pool.memset(ident[:, :], 0.0))
            step(pool.affine_select(out=ident[:, :], in_=ident[:, :], compare_op=ALU.not_equal, fill=1.0,
                                    base=0, pattern=[[-1, P]], channel_multiplier=1))
            step(pool.memset(ones[:, :], 1.0))
            step(pool.memset(causal[:, :], 0.0))
            step(pool.affine_select(out=causal[:, :], in_=causal[:, :], compare_op=ALU.is_ge, fill=NEG,
                                    base=0, pattern=[[-1, P]], channel_multiplier=1))
            step(pool.memset(lower[:, :], 1.0))
            low = lower[:, :].rearrange("p (e j) -> p e j", j=E)
            pool.affine_select(out=low, in_=low, compare_op=ALU.is_gt, fill=0.0,
                               base=0, pattern=[[1, E], [-1, E]], channel_multiplier=0).then_inc(consts_ready, 1)

            with pool.Fori(0, CT // U) as g:
                for s in range(U):
                    pool.wait_ge(hi1_ready, g * U + (s + 1))
                    pool.tensor_tensor(c_lo[:, s % 2, :], ring1[:, s, 0, :], c_hi[:, s % 2, :].bitcast(F32),
                                       ALU.subtract).then_inc(lo1_ready, 1)
            pool.wait_ge(shifted, 1)
            with pool.Fori(1, CT // 2) as m:
                rows = att[:, bass.ds(m * 2, 2), :]
                pool.tensor_tensor(rows, rows, shift[:, :].unsqueeze(1).to_broadcast([P, 2, S]),
                                   ALU.add).then_inc(shifted, 1)
            with pool.Fori(0, GROUPS) as g:
                for j in range(GT):
                    pool.wait_ge(whi_ready, g * GT + (j + 1))
                    pool.tensor_tensor(w_lo[:, j % HL, :, :], raw[:, j, :, :], w_hi[:, j % HL, :, :].bitcast(F32),
                                       ALU.subtract).then_inc(wlo_ready, 1)

        @block.scalar
        def _(act):
            act.dma_start(cols[:, 0:16], cols_in).then_inc(small_loaded, 16)
            act.dma_start(betas[:, :], betas_in.to_broadcast([P, 3])).then_inc(small_loaded, 16)
            act.dma_start(gate[:, :, :], gate_in).then_inc(small_loaded, 16)
            act.dma_start(bv_b[:, :], bv_in.to_broadcast([P, D])).then_inc(small_loaded, 16)

            def root(n, i, st):
                act.wait_ge(var_ready, (n - 1) * ST + i + 1)
                act.activation(std[:, st:st + 1], mv[:, st, 1:2], ACT.Sqrt).then_inc(std_ready, 1)

            def evacuate_lnT(n, i, st, to, bank):
                cut = slice(st * P, (st + 1) * P)
                act.wait_ge(lnT_psum, (n - 1) * ST + i + 1)
                turned = ps[:, bank + st, :].rearrange("p (k c) -> p k c", k=KC)
                act.activation(to[:, :, cut], turned, ACT.Copy).then_inc(lnT_ready, 1)

            for st in range(ST):
                root(1, st, st)
            for d in range(KC):
                act.wait_ge(wqk_psum, d + 1)
                act.activation(wqk[:, d, :], ps[:, d, :], ACT.Copy).then_inc(wqk_ready, 1)
            for st in range(ST):
                evacuate_lnT(1, st, st, lnT_a, 4)
            with act.Fori(0, CT // U) as g:
                for s in range(U):
                    act.wait_ge(s_psum, g * U + (s + 1))
                    act.wait_ge(ring1_full[s], g * 16 + 16)
                    act.activation(c_hi[:, s % 2, :], ring1[:, s, 0, :], ACT.Copy).then_inc(hi1_ready, 1)
            act.wait_ge(s_psum, CT + 2)
            with act.Fori(0, CT // 2 // R2) as g:
                for s in range(R2):
                    m = g * R2 + s
                    act.wait_ge(summed, g * R2 + (s + 1))
                    act.wait_ge(shifted, g * R2 + (s + 1))
                    act.activation(p32[:, s % 2, :, :], att[:, bass.ds(m * 2, 2), :], ACT.Exp).then_inc(exp_done, 1)
                    act.wait_ge(pv_done, g * R2 + (s + 1))
                    act.wait_ge(ring2_full[s], g * 16 + 16)
                    act.activation(d_hi[:, s % 2, :, :], ring2[:, s, :, :], ACT.Copy).then_inc(hi2_ready, 1)
                    act.wait_ge(exp_done, g * R2 + (s + 1))
                    act.activation(p_hi[:, s % 2, :, :], p32[:, s % 2, :, :], ACT.Copy).then_inc(p_hi_ready, 1)

            act.wait_ge(pv_done, CT // 2 + 2)
            act.dma_start(bqkv_b[:, :], bqkv_in.to_broadcast([P, D])).then_inc(bqkv_loaded, 16)
            for k in range(0, KC, 2):
                act.activation(cT[:, k, :], ps[:, 4 + k, :], ACT.Copy).then_inc(cT_even, 1)
            root(2, 0, 0)
            root(2, 1, 1)
            root(2, 2, 2)
            evacuate_lnT(2, 0, 0, lnT, 4)
            root(2, 3, 3)
            for st in range(1, ST):
                evacuate_lnT(2, st, st, lnT, 4)
            for j in range(2 * KC):
                act.wait_ge(qkv_psum, ST + j + 1)
                to = (qT if j < KC else kT)[:, j % KC, :]
                act.activation(to, ps[:, (4 + j) % 8, :], ACT.Identity, bias=cols[:, 8 + j:9 + j]).then_inc(qk2_ready, 1)

            def exponentials(n, i):
                w = (i + 1) * P
                act.wait_ge(nbias_ready, n + 1)
                act.activation(probs[:, i, 0:w], ps[:, 4 + i, 0:w], ACT.Exp, bias=nbias[:, i:i + 1], scale=SCALE,
                               accum_out=rowsum[:, i:i + 1]).then_inc(probs_ready, 1)

            def evacuate_pT(n, i):
                w = (i + 1) * P
                act.wait_ge(pT_psum, n + 1)
                act.activation(pT[:, i, 0:w], ps[:, i, 0:w], ACT.Copy).then_inc(pT_ready, 1)

            for n, i in enumerate(DOWN):
                exponentials(n, i)
                if n >= 1:
                    evacuate_pT(n - 1, DOWN[n - 1])
            evacuate_pT(ST - 1, DOWN[ST - 1])

            def high_parts(g, j):
                act.wait_ge(down_done, g * GT + (j - split_reuse(j) + 1 + CREDIT))
                act.wait_ge(raw_full[j], g * 16 + 16)
                act.activation(w_hi[:, j % HL, :, :], raw[:, j, :, :], ACT.Copy).then_inc(whi_ready, 1)

            def silu(g, j):
                act.wait_ge(g_psum, g * GT + (j + 1))
                act.wait_ge(prod_done, g * GT + (j - pair_reuse(j) + 1 + CREDIT))
                act.activation(gated[:, j % 2, :], ps[:, j % 2, :], ACT.Silu).then_inc(silu_done, 1)

            def group(g, last):
                for j in range(GT):
                    if j + 2 < GT:
                        high_parts(g, j + 2)
                    elif not last:
                        high_parts(g + 1, j + 2 - GT)
                    silu(g, j)

            for n, st in enumerate(DOWN):
                root(3, n, st)
            act.wait_ge(y_psum, ST)
            high_parts(0, 0)
            for n, st in enumerate(DOWN):
                evacuate_lnT(3, n, st, ln3T, 0)
            high_parts(0, 1)
            act.wait_ge(logit_ready, 1)
            act.activation(ex[:, :, 0:E], lg[:, :, 0:E], ACT.Exp).then_inc(gexp_ready, 1)
            act.activation(ex[:, :, E], lg[:, :, E], ACT.Exp, scale=-1.0).then_inc(gexp_ready, 1)
            for m in range(0, WB, 2):
                act.wait_ge(wb_psum, m + 1)
                act.activation(wb[:, m, :], ps[:, WB_BANKS[m % 3], :], ACT.Copy).then_inc(wb_even, 1)
            with act.Fori(0, GROUPS - 1) as g:
                group(g, False)
            group(GROUPS - 1, True)

        @block.tensor
        def _(pe):
            pe.sem_inc(s_psum, 2)
            pe.sem_inc(pv_done, 2)
            pe.sem_inc(down_done, CREDIT)

            def turn_ln(n, i, st, src, bank):
                pe.wait_ge(ln_ready, (n - 1) * ST + i + 1)
                for k in range(KC):
                    mm = pe.transpose(ps[:, bank + st, k * P:(k + 1) * P], src[:, st, k * P:(k + 1) * P],
                                      ident[:, :])
                mm.then_inc(lnT_psum, 1)

            def product(bank, width, lhs, rhs, terms):
                for k in range(terms):
                    mm = pe.matmul(ps[:, bank, 0:width], lhs(k), rhs(k), start=(k == 0), stop=(k == terms - 1))
                return mm

            def open_sums():
                for b in range(4, 8):
                    for q in range(4):
                        pe.matmul(ps[:, b, q * P:(q + 1) * P], zero16[:, :], zero16[:, :], start=(q == 0), stop=False,
                                  skip_group_check=True)

            pe.wait_ge(wqk_loaded, 32)
            for d in range(KC):
                product(d, D, lambda k: wq[:, k, d * P:(d + 1) * P], lambda k: wk[:, k, :], KC).then_inc(wqk_psum, 1)
            pe.wait_ge(small_loaded, 64)
            pe.wait_ge(bkb_ready, 1)
            pe.wait_ge(wqk_ready, 1)
            for d in range(KC):
                for c, w, b in ((d, wk, 0), (KC + d, wq, KC)):
                    for k in range(KC):
                        pe.matmul(ps[:, 0, c:c + 1], w[:, k, d * P:(d + 1) * P], cols[:, b + k:b + k + 1],
                                  start=(k == 0), stop=(k == KC - 1))
            for k in range(KC):
                mm = pe.matmul(ps[:, 0, 2 * KC:2 * KC + 1], bkb[:, k, :], cols[:, k:k + 1],
                               start=(k == 0), stop=(k == KC - 1))
            mm.then_inc(bias_psum, 1)
            pe.wait_ge(consts_ready, 1)
            for st in range(ST):
                turn_ln(1, st, st, ln_a, 4)
            pe.wait_ge(lnT_ready, ST)
            pe.wait_ge(wqk_ready, KC)
            for d in range(KC):
                product(4 + d, S, lambda k: wqk[:, k, d * P:(d + 1) * P], lambda k: lnT_a[:, k, :], KC).then_inc(qk_psum, 1)
            pe.wait_ge(ub_ready, 1)
            product(3, S, lambda k: ub[:, k, :], lambda k: lnT_a[:, k, :], KC).then_inc(qb_psum, 1)
            pe.wait_ge(qk_ready, KC + 1)

            with pe.Fori(0, CT // U) as g:
                for s in range(U):
                    pe.wait_ge(hi1_ready, g * U + (s + 1))
                    pe.wait_ge(att_ready, g * U + (s + 1))
                    for k in range(KC):
                        hi = c_hi[:, s % 2, k * P:(k + 1) * P]
                        pe.matmul(ps[:, s, :], hi, qk_hi[:, k, :], start=(k == 0), stop=False)
                        pe.matmul(ps[:, s, :], hi, qk_lo[:, k, :], start=False, stop=False)
                    pe.wait_ge(lo1_ready, g * U + (s + 1))
                    for k in range(KC):
                        mm = pe.matmul(ps[:, s, :], c_lo[:, s % 2, k * P:(k + 1) * P], qk_hi[:, k, :],
                                       start=False, stop=(k == KC - 1))
                    mm.then_inc(s_psum, 1)
            pe.wait_ge(max_done, CT + 1)
            for q in range(ST):
                mm = pe.transpose(ps[:, 0, q * P:(q + 1) * P], runmax[:, q * P:(q + 1) * P], ident[:, :])
            mm.then_inc(maxT_psum, 1)
            pe.wait_ge(diag_ready, 1)
            for q in range(ST):
                mm = pe.matmul(ps[:, 1, q * P:(q + 1) * P], ones[:, :], diag[:, q, :], start=True, stop=True)
            mm.then_inc(maxb_psum, 1)

            open_sums()
            with pe.Fori(0, CT // 2 // R2) as g:
                for s in range(R2):
                    m = g * R2 + (s + 1)
                    slot = s % 2

                    def add(a, b):
                        for t in range(2):
                            for d in range(KC):
                                mm = pe.matmul(ps[:, 4 + d, :], a[:, slot, t, d * P:(d + 1) * P], b[:, slot, t, :],
                                               start=False, stop=False, skip_group_check=True)
                        return mm

                    pe.wait_ge(hi2_ready, m)
                    pe.wait_ge(p_hi_ready, m)
                    add(d_hi, p_hi)
                    pe.wait_ge(lo2_ready, m)
                    add(d_lo, p_hi)
                    pe.wait_ge(p_lo_ready, m)
                    add(d_hi, p_lo).then_inc(pv_done, 1)
            pe.wait_ge(summed, CT // 2 + 2)
            for st in range(ST):
                for t in range(2):
                    mm = pe.matmul(ps[:, 3, st:st + 1], expsum[:, t, st * P:(st + 1) * P], ones[:, 0:1],
                                   start=(t == 0), stop=(t == 1))
            mm.then_inc(sum_psum, 1)
            pe.wait_ge(wv_loaded, 16)
            pe.wait_ge(cT_even, KC // 2)
            pe.wait_ge(cT_odd, KC // 2)
            for st in range(ST):
                if st == ST - 1:
                    pe.wait_ge(sum_read, 1)
                product(st, D, lambda k: cT[:, k, st * P:(st + 1) * P], lambda k: wv[:, k, :], KC).then_inc(o_psum, 1)

            pe.wait_ge(wqkv_loaded, 16)

            def value(st):
                pe.wait_ge(lnT_ready, ST + st + 1)
                product(st, D, lambda k: lnT[:, k, st * P:(st + 1) * P], lambda k: wqkv[:, k, 2 * D:3 * D],
                        KC).then_inc(qkv_psum, 1)

            for st in range(ST):
                turn_ln(2, st, st, ln, 4)
                if st >= 1:
                    value(st - 1)
            value(ST - 1)
            for j in range(2 * KC):
                if j >= KC:
                    pe.wait_ge(v_ready, j - KC + 1)
                product((4 + j) % 8, S, lambda k: wqkv[:, k, j * P:(j + 1) * P], lambda k: lnT[:, k, :],
                        KC).then_inc(qkv_psum, 1)
            pe.wait_ge(qk2_ready, 2 * KC)
            for i in DOWN:
                w = (i + 1) * P
                product(4 + i, w, lambda k: qT[:, k, i * P:(i + 1) * P], lambda k: kT[:, k, 0:w], KC).then_inc(sc_psum, 1)

            def turn_probs(n, i):
                pe.wait_ge(probs_ready, n + 1)
                for k in range(i + 1):
                    mm = pe.transpose(ps[:, i, k * P:(k + 1) * P], probs[:, i, k * P:(k + 1) * P], ident[:, :])
                mm.then_inc(pT_psum, 1)

            def attend(n, i):
                pe.wait_ge(pT_ready, n + 1)
                product(4 + i, D, lambda k: pT[:, i, k * P:(k + 1) * P], lambda k: v[:, k, :], i + 1).then_inc(y_psum, 1)

            for n, i in enumerate(DOWN):
                turn_probs(n, i)
                if n >= 1:
                    attend(n - 1, DOWN[n - 1])
            attend(ST - 1, DOWN[ST - 1])

            for n, st in enumerate(DOWN):
                turn_ln(3, n, st, ln, 0)
            for n, st in enumerate(DOWN):
                pe.wait_ge(lnT_ready, 2 * ST + n + 1)
                for k in range(KC):
                    mm = pe.matmul(ps[:, 4, 16 * st:16 * st + E + 1], ln3T[:, k, st * P:(st + 1) * P], gate[:, k, :],
                                   start=(k == 0), stop=(k == KC - 1))
            mm.then_inc(logit_psum, 1)

            def up(g, j):
                n = g * GT
                pe.wait_ge(whi_ready, n + (j + 1))
                pe.wait_ge(wlo_ready, n + (j + 1))
                pe.wait_ge(prod_done, n + (j - pair_reuse(j) + 1 + CREDIT))
                for part, bank, done in ((0, j % 2, g_psum), (1, 2 + j % 2, u_psum)):
                    for k in range(KC):
                        hi, lo = (w[:, j % HL, part, k * P:(k + 1) * P] for w in (w_hi, w_lo))
                        pe.matmul(ps[:, bank, :], hi, l_hi[:, k, :], start=(k == 0), stop=False)
                        pe.matmul(ps[:, bank, :], hi, l_lo[:, k, :], start=False, stop=False)
                        mm = pe.matmul(ps[:, bank, :], lo, l_hi[:, k, :], start=False, stop=(k == KC - 1))
                    mm.then_inc(done, 1)

            def down(g, j):
                pe.wait_ge(h_ready, g * GT + (j + 1))
                for st in range(ST):
                    hi, lo = (h[:, j % 2, st * P:(st + 1) * P] for h in (h_hi, h_lo))
                    for a, b in ((hi, w_hi), (hi, w_lo), (lo, w_hi)):
                        mm = pe.matmul(ps[:, 4 + st, :], a, b[:, j % HL, 2, :], start=False, stop=False,
                                       skip_group_check=True)
                mm.then_inc(down_done, 1)

            pe.wait_ge(split3_ready, KC)
            up(0, 0)
            pe.wait_ge(wn_ready, 1)
            for st in range(ST):
                mm = pe.matmul(ps[0:E + 1, 5, st * P:(st + 1) * P], wn[:, st, :], ident[:, :], start=True, stop=True)
            mm.then_inc(wT_psum, 1)
            pe.wait_ge(wT_ready, 1)
            for m in range(WB):
                if m >= 3:
                    pe.wait_ge(*((wb_odd, (m - 3) // 2 + 1) if m % 2 == 0 else (wb_even, (m - 3) // 2 + 1)))
                bank = ps[:, WB_BANKS[m % 3], :]
                pe.matmul(bank, sel[0:E + 1, m, :], wT_hi[0:E + 1, :], start=True, stop=False)
                pe.matmul(bank, sel[0:E + 1, m, :], wT_lo[0:E + 1, :], start=False, stop=True).then_inc(wb_psum, 1)
            pe.wait_ge(wb_even, (WB + 1) // 2)
            pe.wait_ge(wb_odd, WB // 2)
            open_sums()

            def group(g, last):
                for j in range(GT):
                    if j + 1 < GT:
                        up(g, j + 1)
                    elif not last:
                        up(g + 1, 0)
                    down(g, j)

            with pe.Fori(0, GROUPS - 1) as g:
                group(g, False)
            group(GROUPS - 1, True)

        @block.vector
        def _(dve):
            steps = [0]

            def step(ins):
                steps[0] += 1
                ins.then_inc(dve_step, 1)
                dve.wait_ge(dve_step, steps[0])

            def moments(st):
                step(dve.bn_stats(stats[:, st, :], x[:, st, :]))
                step(dve.bn_aggr(mv[:, st, :], stats[:, st, :]))
                dve.tensor_scalar(mv[:, st, 1:2], mv[:, st, 1:2], EPS, None, ALU.add).then_inc(var_ready, 1)

            def normalize(n, i, st, to):
                dve.wait_ge(std_ready, (n - 1) * ST + i + 1)
                step(dve.reciprocal(rstd[:, st:st + 1], std[:, st:st + 1]))
                dve.tensor_scalar(to[:, st, :], x[:, st, :], mv[:, st, 0:1], rstd[:, st:st + 1],
                                  ALU.subtract, ALU.mult).then_inc(ln_ready, 1)

            dve.sem_inc(att_ready, SB)
            dve.sem_inc(summed, 2)
            dve.sem_inc(prod_done, CREDIT)
            dve.wait_ge(x_loaded, 16)
            for st in range(ST):
                moments(st)
                if st >= 1:
                    normalize(1, st - 1, st - 1, ln_a)
            normalize(1, ST - 1, ST - 1, ln_a)
            dve.wait_ge(consts_ready, 1)
            dve.wait_ge(small_loaded, 64)
            for k in range(KC):
                ins = dve.tensor_scalar(bkb[:, k, :], ones[:, :], cols[:, 4 + k:5 + k], None, ALU.mult)
            ins.then_inc(bkb_ready, 1)
            dve.wait_ge(ln_ready, ST)
            for st in range(ST):
                ins = dve.tensor_tensor(x[:, st, :], x[:, st, :], bv_b[:, :], ALU.add)
            step(ins)
            step(dve.tensor_tensor(beta[:, :], betas[:, 0:1], betas[:, 1:2], ALU.add))
            step(dve.tensor_tensor(beta[:, :], beta[:, :], betas[:, 2:3], ALU.subtract))
            dve.memset(zero16[:, :], 0.0)
            dve.memset(runmax[:, :], -3.0e38).then_inc(max_done, 1)
            dve.wait_ge(bias_psum, 1)
            step(dve.tensor_copy(cbias[:, :], ps[:, 0, 0:2 * KC + 1]))
            for k in range(KC):
                ins = dve.tensor_scalar(ub[:, k, :], ones[:, :], cbias[:, KC + k:KC + k + 1], None, ALU.mult)
            ins.then_inc(ub_ready, 1)
            for d in range(KC):
                dve.wait_ge(qk_psum, d + 1)
                step(dve.tensor_scalar(qk32[:, d, :], ps[:, 4 + d, :], cbias[:, d:d + 1], SCALE, ALU.add, ALU.mult))
                step(dve.tensor_copy(qk_hi[:, d, :], qk32[:, d, :]))
                dve.tensor_tensor(qk_lo[:, d, :], qk32[:, d, :], qk_hi[:, d, :].bitcast(F32),
                                  ALU.subtract).then_inc(qk_ready, 1)
            dve.wait_ge(qb_psum, 1)
            dve.tensor_scalar(qb[:, :], ps[:, 3, :], cbias[:, 2 * KC:2 * KC + 1], SCALE, ALU.add,
                              ALU.mult).then_inc(qk_ready, 1)

            with dve.Fori(0, CT // U) as g:
                for s in range(U):
                    dve.wait_ge(s_psum, g * U + (s + 1 + 2))
                    dve.scalar_tensor_tensor(out=att[:, g * U + s, :], in0=ring1[:, s, 1, :], scalar=beta[:, 0:1],
                                             in1=ps[:, s, :], op0=ALU.mult, op1=ALU.add).then_inc(att_ready, 1)
                    dve.wait_ge(att_ready, g * U + (s + 1 + SB))
                    dve.wait_ge(max_done, g * U + (s + 1))
                    dve.tensor_tensor(runmax[:, :], runmax[:, :], att[:, g * U + s, :], ALU.max).then_inc(max_done, 1)
            dve.wait_ge(maxT_psum, 1)
            step(dve.tensor_reduce(mcol[:, :], ps[:, 0, :].rearrange("p (q c) -> p q c", q=ST), AX_X, ALU.max))
            for q in range(ST):
                ins = dve.tensor_scalar(diag[:, q, :], ident[:, :], mcol[:, q:q + 1], None, ALU.mult)
            ins.then_inc(diag_ready, 1)
            dve.wait_ge(maxb_psum, 1)
            step(dve.tensor_tensor(shift_t[:, :], ps[:, 1, :], qb[:, :], ALU.add))
            dve.tensor_tensor(shift[:, :], qb[:, :], shift_t[:, :], ALU.subtract).then_inc(shift_ready, 1)
            dve.wait_ge(shift_ready, 1)
            dve.tensor_tensor(att[:, 0:2, :], att[:, 0:2, :], shift[:, :].unsqueeze(1).to_broadcast([P, 2, S]),
                              ALU.add).then_inc(shifted, 1)
            step(dve.memset(expsum[:, :, :], 0.0))
            with dve.Fori(0, CT // 2 // R2) as g:
                for s in range(R2):
                    m = g * R2 + (s + 1)
                    slot = s % 2
                    dve.wait_ge(hi2_ready, m)
                    dve.tensor_tensor(d_lo[:, slot, :, :], ring2[:, s, :, :], d_hi[:, slot, :, :].bitcast(F32),
                                      ALU.subtract).then_inc(lo2_ready, 1)
                    dve.wait_ge(p_hi_ready, m)
                    dve.tensor_tensor(p_lo[:, slot, :, :], p32[:, slot, :, :], p_hi[:, slot, :, :].bitcast(F32),
                                      ALU.subtract).then_inc(p_lo_ready, 1)
                    dve.wait_ge(summed, g * R2 + (s + 2))
                    dve.tensor_tensor(expsum[:, :, :], expsum[:, :, :], p32[:, slot, :, :], ALU.add).then_inc(summed, 1)
            dve.wait_ge(pv_done, CT // 2 + 2)
            for k in range(1, KC, 2):
                dve.tensor_copy(cT[:, k, :], ps[:, 4 + k, :]).then_inc(cT_odd, 1)
            dve.wait_ge(sum_psum, 1)
            dve.reciprocal(rinv[:, :], ps[:, 3, 0:ST]).then_inc(sum_read, 1)
            dve.wait_ge(sum_read, 1)
            for st in range(ST):
                dve.wait_ge(o_psum, st + 1)
                step(dve.scalar_tensor_tensor(out=x[:, st, :], in0=ps[:, st, :], scalar=rinv[:, st:st + 1],
                                              in1=x[:, st, :], op0=ALU.mult, op1=ALU.add))
                moments(st)
                if st >= 1:
                    normalize(2, st - 1, st - 1, ln)
            normalize(2, ST - 1, ST - 1, ln)

            dve.wait_ge(bqkv_loaded, 16)
            for st in range(ST):
                dve.wait_ge(qkv_psum, st + 1)
                dve.tensor_tensor(v[:, st, :], ps[:, st, :], bqkv_b[:, :], ALU.add).then_inc(v_ready, 1)
            for n, i in enumerate(DOWN):
                w = (i + 1) * P
                dve.wait_ge(sc_psum, n + 1)
                step(dve.tensor_tensor(ps[:, 4 + i, i * P:w], ps[:, 4 + i, i * P:w], causal[:, :], ALU.add))
                step(dve.tensor_reduce(mcol[:, i:i + 1], ps[:, 4 + i, 0:w], AX_X, ALU.max))
                dve.tensor_scalar(nbias[:, i:i + 1], mcol[:, i:i + 1], -SCALE, None, ALU.mult).then_inc(nbias_ready, 1)
            for n, i in enumerate(DOWN):
                dve.wait_ge(probs_ready, n + 1)
                step(dve.reciprocal(rinv[:, i:i + 1], rowsum[:, i:i + 1]))
                dve.wait_ge(y_psum, n + 1)
                step(dve.scalar_tensor_tensor(out=x[:, i, :], in0=ps[:, 4 + i, :], scalar=rinv[:, i:i + 1],
                                              in1=x[:, i, :], op0=ALU.mult, op1=ALU.add))
                moments(i)
                if n >= 1:
                    normalize(3, n - 1, DOWN[n - 1], ln)
            normalize(3, ST - 1, DOWN[ST - 1], ln)

            for n, st in enumerate(DOWN):
                cut = slice(st * P, (st + 1) * P)
                dve.wait_ge(lnT_ready, 2 * ST + n + 1)
                step(dve.tensor_copy(l_hi[:, :, cut], ln3T[:, :, cut]))
                dve.tensor_tensor(l_lo[:, :, cut], ln3T[:, :, cut], l_hi[:, :, cut].bitcast(F32),
                                  ALU.subtract).then_inc(split3_ready, 1)
            dve.wait_ge(logit_psum, 1)
            step(dve.tensor_copy(lg[:, :, :], ps[:, 4, 0:16 * ST].rearrange("p (t c) -> p t c", c=16)[:, :, 0:E + 1]))
            le = lg[:, :, 0:E]
            step(dve.tensor_reduce(mcol[:, :], le, AX_X, ALU.max))
            step(dve.tensor_tensor(le, le, mcol[:, :].unsqueeze(2).to_broadcast([P, ST, E]), ALU.subtract))
            dve.sem_inc(logit_ready, 1)
            other = le.unsqueeze(2).to_broadcast([P, ST, E, E])
            own = le.unsqueeze(3).to_broadcast([P, ST, E, E])
            gt = cmp_gt[:, :, :].rearrange("p t (e j) -> p t e j", j=E)
            ge = cmp_ge[:, :, :].rearrange("p t (e j) -> p t e j", j=E)
            dve.tensor_tensor(gt, other, own, ALU.is_gt)
            step(dve.tensor_tensor(ge, other, own, ALU.is_ge))
            step(dve.tensor_tensor(cmp_ge[:, :, :], cmp_ge[:, :, :],
                                   lower[:, :].unsqueeze(1).to_broadcast([P, ST, E * E]), ALU.mult))
            step(dve.tensor_tensor(cmp_gt[:, :, :], cmp_gt[:, :, :], cmp_ge[:, :, :], ALU.max))
            step(dve.tensor_reduce(rank[:, :, :], gt, AX_X, ALU.add))
            dve.wait_ge(gexp_ready, 2)
            step(dve.tensor_reduce(rowsum[:, :], ex[:, :, 0:E], AX_X, ALU.add))
            step(dve.reciprocal(rinv[:, :], rowsum[:, :]))
            dve.tensor_scalar(ex[:, :, E], ex[:, :, E], 1.0, None, ALU.add)
            step(dve.scalar_tensor_tensor(out=wn[:, :, 0:E], in0=rank[:, :, :], scalar=2.0, in1=ex[:, :, 0:E],
                                          op0=ALU.is_lt, op1=ALU.mult))
            dve.reciprocal(wn[:, :, E], ex[:, :, E])
            step(dve.tensor_tensor(wn[:, :, 0:E], wn[:, :, 0:E], rinv[:, :].unsqueeze(2).to_broadcast([P, ST, E]),
                                   ALU.mult))
            dve.sem_inc(wn_ready, 1)
            unit = ident[0:E + 1, 0:E + 1]
            pairs = sel[0:E + 1, 0:WB - 1, :].rearrange("p (g a) c -> p g a c", a=3)
            for par in range(2):
                col = unit[:, par:E:2].unsqueeze(2)
                dve.tensor_copy(pairs[:, :, 2 * par, :], col.to_broadcast([E + 1, E // 2, P]))
                ins = dve.tensor_copy(pairs[:, :, 1, par * 64:par * 64 + 64], col.to_broadcast([E + 1, E // 2, 64]))
            step(dve.tensor_copy(sel[0:E + 1, WB - 1, :], unit[:, E:E + 1].to_broadcast([E + 1, P])))
            dve.wait_ge(wT_psum, 1)
            step(dve.tensor_copy(wT_hi[0:E + 1, :], ps[0:E + 1, 5, :]))
            dve.tensor_tensor(wT_lo[0:E + 1, :], ps[0:E + 1, 5, :], wT_hi[0:E + 1, :].bitcast(F32),
                              ALU.subtract).then_inc(wT_ready, 1)
            for m in range(1, WB, 2):
                dve.wait_ge(wb_psum, m + 1)
                dve.tensor_copy(wb[:, m, :], ps[:, WB_BANKS[m % 3], :]).then_inc(wb_odd, 1)
            dve.wait_ge(wb_even, (WB + 1) // 2)
            dve.wait_ge(wb_odd, WB // 2)

            def hidden(g, j, weight):
                n = g * GT
                dve.wait_ge(silu_done, n + (j + 1))
                dve.wait_ge(u_psum, n + (j + 1))
                dve.wait_ge(down_done, n + (j - pair_reuse(j) + 1 + CREDIT))
                dve.tensor_tensor(hid32[:, j % 2, :], gated[:, j % 2, :], ps[:, 2 + j % 2, :],
                                  ALU.mult).then_inc(prod_done, 1)
                dve.wait_ge(prod_done, n + (j + 1 + CREDIT))
                dve.tensor_tensor(hid32[:, j % 2, :], hid32[:, j % 2, :], weight, ALU.mult).then_inc(hid_done, 1)
                dve.wait_ge(hid_done, n + (j + 1))
                dve.tensor_copy(h_hi[:, j % 2, :], hid32[:, j % 2, :]).then_inc(hhi_ready, 1)
                dve.wait_ge(hhi_ready, n + (j + 1))
                dve.tensor_tensor(h_lo[:, j % 2, :], hid32[:, j % 2, :], h_hi[:, j % 2, :].bitcast(F32),
                                  ALU.subtract).then_inc(h_ready, 1)

            with dve.Fori(0, GROUPS - 1) as g:
                for j in range(GT):
                    kind = 0 if j < MIX else 1 if j == MIX else 2
                    hidden(g, j, wb[:, g * 3 + kind, :])
            for j in range(GT):
                hidden(GROUPS - 1, j, wb[:, WB - 1, :])
            dve.wait_ge(down_done, GROUPS * GT + CREDIT)
            for st in range(ST):
                dve.tensor_tensor(x[:, st, :], x[:, st, :], ps[:, 4 + st, :], ALU.add).then_inc(y_ready, 1)


def kernel(x, ctx_1024, fside_BxSxS2_0, L0_xattn_Wq, L0_xattn_bq, L0_xattn_Wk, L0_xattn_bk, L0_xattn_Wv, L0_xattn_bv,
           L0_xattn_beta_risk, L0_xattn_beta_prio, L0_xattn_beta_impl, L0_attn_W_qkv, L0_attn_b_qkv, L0_ffn_gate_w,
           L0_ffn_experts_gate_up, L0_ffn_experts_down, L0_ffn_shared_gate_w, L0_ffn_shared_up_w,
           L0_ffn_shared_down_w, L0_ffn_shared_expert_gate_w):
    import numpy as np
    import concourse.bacc as bacc
    from concourse.bass_utils import run_bass_kernel_spmd

    def rows(w):
        w = np.asarray(w)
        return w.reshape(w.shape[0] // P, P, w.shape[1]).transpose(1, 0, 2)

    def columns(b):
        return np.asarray(b).reshape(-1, P).T

    ctx = np.asarray(ctx_1024)[0].reshape(CT, P, KC, P)
    fside = np.asarray(fside_BxSxS2_0)[0]
    stream1 = np.stack([ctx.transpose(0, 3, 2, 1).reshape(CT, P, D), fside.T.reshape(CT, P, S)], axis=2)

    gu = np.asarray(L0_ffn_experts_gate_up)
    gate_rows = np.concatenate([gu[:, :NI].reshape(-1, D), np.asarray(L0_ffn_shared_gate_w)])
    up_rows = np.concatenate([gu[:, NI:].reshape(-1, D), np.asarray(L0_ffn_shared_up_w)])
    down_rows = np.concatenate([np.asarray(L0_ffn_experts_down).transpose(0, 2, 1).reshape(-1, D),
                                np.asarray(L0_ffn_shared_down_w).T])
    tiles = GROUPS * GT

    def turned(w):
        return w.reshape(tiles, P, KC, P).transpose(0, 3, 2, 1).reshape(tiles, P, D)

    b_qkv = np.asarray(L0_attn_b_qkv)
    given = {
        "x_in": np.asarray(x)[0],
        "stream1": stream1,
        "ctx_in": ctx.reshape(CT // 2, 2, P, D).transpose(0, 2, 1, 3),
        "wq_in": rows(L0_xattn_Wq),
        "wk_in": rows(L0_xattn_Wk),
        "wv_in": rows(np.asarray(L0_xattn_Wv).T),
        "wqkv_in": rows(np.asarray(L0_attn_W_qkv).T),
        "gate_in": rows(np.concatenate([np.asarray(L0_ffn_gate_w), np.asarray(L0_ffn_shared_expert_gate_w)]).T),
        "ffn_in": np.stack([turned(gate_rows), turned(up_rows), down_rows.reshape(tiles, P, D)], axis=2),
        "cols_in": np.concatenate([columns(L0_xattn_bq), columns(L0_xattn_bk), columns(b_qkv[:2 * D])], axis=1),
        "bv_in": np.asarray(L0_xattn_bv).reshape(1, D),
        "bqkv_in": b_qkv[2 * D:].reshape(1, D),
        "betas_in": np.stack([np.asarray(L0_xattn_beta_risk), np.asarray(L0_xattn_beta_prio),
                              np.asarray(L0_xattn_beta_impl)]).reshape(1, 3),
    }
    given = {name: np.ascontiguousarray(a) for name, a in given.items()}
    nc = bacc.Bacc("TRN2", target_bir_lowering=False, num_devices=1)
    args = {name: nc.dram_tensor(name, a.shape, mybir.dt.from_np(a.dtype), kind="ExternalInput").ap()
            for name, a in given.items()}
    result = nc.dram_tensor("result", (S, D), F32, kind="ExternalOutput").ap()
    perceiver_layer(nc, out=result, **args)
    r = run_bass_kernel_spmd(nc, [given], core_ids=[0])
    return r.results[0]["result"].reshape(1, S, D)
```

```python
from contextlib import ExitStack

import concourse.bass as bass
from concourse import mybir

F32 = mybir.dt.float32
F32R = mybir.dt.float32r
ALU = mybir.AluOpType
ACT = mybir.ActivationFunctionType
AX_X = mybir.AxisListType.X

P = 128
D = 512
S = 512
T = 8192
KC = D // P
ST = S // P
CT = T // P
U = 4
E = 8
NI = 704
SH = 11
ET = 6
HALF = NI - (ET - 1) * P
CAP = 256
MORE = 3
NU = E + MORE
RAW = 6
FAR = 1024.0
EPS = 1e-5
SCALE = float(D) ** -0.5
NEG = -1.0e30
HL = 3
R2 = 4
DOWN = tuple(reversed(range(ST)))
SB = 4
CREDIT = 3


def perceiver_layer(nc, x_in, stream1, ctx_in, wq_in, wk_in, wv_in, wqkv_in, gate_in, shared_in, full_in,
                    half_up_in, half_down_in,
                    cols_in, bv_in, bqkv_in, betas_in, out):
    with ExitStack() as scope:
        KB = 1024
        base = 16512

        def at(name, shape, dt, kb):
            return nc.alloc_sbuf_tensor_at(name, shape, dt, offset=base + int(kb * KB))

        def sem(name):
            return scope.enter_context(nc.semaphore(name))

        x = at("x", [P, ST, D], F32, 0)
        ident = at("ident", [P, P], F32, 8)
        ones = at("ones", [P, P], F32, 8.5)
        causal = at("causal", [P, P], F32, 9)
        lower = at("lower", [P, E * E], F32, 9.5)
        gate = at("gate", [P, KC, E + 1], F32, 9.75)
        cols = at("cols", [P, 20], F32, 10)
        stats = at("stats", [P, ST, 6], F32, 10.125)
        mv = at("mv", [P, ST, 2], F32, 10.25)
        std = at("std", [P, ST], F32, 10.3125)
        rstd = at("rstd", [P, ST], F32, 10.34375)
        beta = at("beta", [P, 1], F32, 10.375)
        mcol = at("mcol", [P, ST], F32, 10.40625)
        nbias = at("nbias", [P, ST], F32, 10.4375)
        rowsum = at("rowsum", [P, ST], F32, 10.46875)
        rinv = at("rinv", [P, ST], F32, 10.5)
        betas = at("betas", [P, 3], F32, 10.53125)
        lg = at("lg", [P, ST, E + 1], F32, 10.5625)
        ex = at("ex", [P, ST, E + 1], F32, 10.75)
        wn = at("wn", [P, ST, NU], F32, 11)
        rank = at("rank", [P, ST, E], F32, 11.25)
        taken = at("taken", [P, ST, E], F32, 11.375)
        zero16 = at("zero16", [P, P], mybir.dt.bfloat16, 11.5)
        place = at("place", [P, ST, NU], F32, 11.75)
        qk_hi = at("qk_hi", [P, KC, S], F32R, 12)
        qk_lo = at("qk_lo", [P, KC, S], F32R, 20)
        runmax = at("runmax", [P, S], F32, 28)
        shift = at("shift", [P, S], F32, 30)
        ring1 = at("ring1", [P, U, 2, D], F32, 32)
        ring2 = at("ring2", [P, R2, 2, D], F32, 48)
        c_hi = at("c_hi", [P, 2, D], F32R, 68)
        c_lo = at("c_lo", [P, 2, D], F32R, 72)
        d_hi = at("d_hi", [P, 2, 2, D], F32R, 12)
        d_lo = at("d_lo", [P, 2, 2, D], F32R, 20)
        p32 = at("p32", [P, 2, 2, S], F32, 32)
        p_hi = at("p_hi", [P, 2, 2, S], F32R, 40)
        p_lo = at("p_lo", [P, 2, 2, S], F32R, 64)
        expsum = at("expsum", [P, 2, S], F32, 72)
        att = at("att", [P, CT, S], F32, 76)
        qb = at("qb", [P, S], F32, 204)
        wq_hi = at("wq_hi", [P, KC, D], F32R, 76)
        wq_lo = at("wq_lo", [P, KC, D], F32R, 84)
        wk_hi = at("wk_hi", [P, KC, D], F32R, 92)
        wk_lo = at("wk_lo", [P, KC, D], F32R, 100)
        wq = at("wq", [P, KC, D], F32, 116)
        wk = at("wk", [P, KC, D], F32, 124)
        ln_a = at("ln_a", [P, ST, D], F32, 132)
        lna_hi = at("lna_hi", [P, KC, S], F32R, 140)
        lna_lo = at("lna_lo", [P, KC, S], F32R, 148)
        q32 = at("q32", [P, KC, S], F32, 156)
        q_hi = at("q_hi", [P, KC, S], F32R, 164)
        q_lo = at("q_lo", [P, KC, S], F32R, 172)
        qk32 = at("qk32", [P, KC, S], F32, 180)
        bkb = at("bkb", [P, KC, P], F32, 188)
        bkb_hi = at("bkb_hi", [P, KC, P], F32R, 190)
        bkb_lo = at("bkb_lo", [P, KC, P], F32R, 192)
        bv_b = at("bv_b", [P, D], F32, 194)
        shift_t = at("shift_t", [P, S], F32, 32)
        diag = at("diag", [P, ST, P], F32, 34)
        wqkv = at("wqkv", [P, KC, 3 * D], F32, 76)
        wv = at("wv", [P, KC, D], F32, 100)
        wqkv_hi = at("wqkv_hi", [P, KC, 3 * D], F32R, 108)
        wqkv_lo = at("wqkv_lo", [P, KC, 3 * D], F32R, 132)
        wv_hi = at("wv_hi", [P, KC, D], F32R, 156)
        wv_lo = at("wv_lo", [P, KC, D], F32R, 164)
        ln = at("ln", [P, ST, D], F32, 174)
        lnT_hi = at("lnT_hi", [P, KC, S], F32R, 182)
        lnT_lo = at("lnT_lo", [P, KC, S], F32R, 64)
        cT_hi = at("cT_hi", [P, KC, S], F32R, 190)
        cT_lo = at("cT_lo", [P, KC, S], F32R, 56)
        qT = at("qT", [P, KC, S], F32, 12)
        kT = at("kT", [P, KC, S], F32, 20)
        v = at("v", [P, ST, D], F32, 32)
        probs = at("probs", [P, ST, S], F32, 40)
        pT = at("pT", [P, ST, S], F32, 48)
        bqkv_b = at("bqkv_b", [P, D], F32, 198)
        w_hi = at("w_hi", [P, HL, 3, D], F32R, 12)
        w_lo = at("w_lo", [P, HL, 3, D], F32R, 30)
        h_hi = at("h_hi", [P, 2, S], F32R, 48)
        h_lo = at("h_lo", [P, 2, S], F32R, 52)
        gated = at("gated", [P, 2, S], F32, 56)
        hid32 = at("hid32", [P, 2, S], F32, 60)
        ln3T = at("ln3T", [P, KC, S], F32, 64)
        raw = at("raw", [P, RAW, 3, D], F32, 72)
        pick = at("pick", [P, NU * ST, CAP], F32R, 108)
        t_hi = at("t_hi", [P, ST, D], F32R, 152)
        t_lo = at("t_lo", [P, ST, D], F32R, 160)
        y_hi = at("y_hi", [P, 2, D], F32R, 174)
        y_lo = at("y_lo", [P, 2, D], F32R, 178)
        wb = at("wb", [P, S], F32, 172)
        l_hi = at("l_hi", [P, KC, S], F32R, 182)
        l_lo = at("l_lo", [P, KC, S], F32R, 190)
        xg_hi = at("xg_hi", [P, KC, CAP], F32R, 182)
        back = at("back", [P, 2, S], F32R, 186)
        xg_lo = at("xg_lo", [P, KC, CAP], F32R, 190)
        ones_r = at("ones_r", [P, P], F32R, 198)
        own_places = at("own_places", [P, S], F32R, 199)
        before = at("before", [P, P], F32, 202.5)
        places_t = at("places_t", [P, S], F32, 203)
        cmp_gt = at("cmp_gt", [P, ST, E * E], F32, 64)
        cmp_ge = at("cmp_ge", [P, ST, E * E], F32, 65)
        up_half = at("up_half", [HALF, CAP], F32, 64)
        slot_col = at("slot_col", [P, 2], F32, 66)
        most = at("most", [P, 1], F32, 66.0625)
        more = at("more", [P, 1], mybir.dt.int32, 66.125)
        which = at("which", [P, MORE], mybir.dt.int32, 66.1875)
        over = at("over", [P, E], F32, 66.25)
        over_rank = at("over_rank", [P, E], F32, 66.375)
        over_hot = at("over_hot", [P, MORE, E], F32, 66.5)
        which32 = at("which32", [P, MORE], F32, 66.625)
        slot_row = at("slot_row", [P, CAP], F32, 67)
        gate_diag = at("gate_diag", [P, ST, P], F32, 68)
        scratch = at("scratch", [P, ST, MORE, E], F32, 70)
        gate_col = at("gate_col", [P, ST], F32, 71)

        ps = scope.enter_context(nc.psum_tensor("ps", [P, 8, 512], F32))

        wq_loaded, wk_loaded, small_loaded = sem("wq_loaded"), sem("wk_loaded"), sem("small_loaded")
        wv_loaded, wqkv_loaded, bqkv_loaded, out_stored = sem("wv_loaded"), sem("wqkv_loaded"), sem("bqkv_loaded"), sem("out_stored")
        x_loaded = [sem(f"x_loaded{st}") for st in range(ST)]
        ring1_full = [sem(f"ring1_full{s}") for s in range(U)]
        ring2_full = [sem(f"ring2_full{s}") for s in range(R2)]
        raw_full = [sem(f"raw_full{s}") for s in range(RAW)]
        pool_step, dve_step = sem("pool_step"), sem("dve_step")
        consts_ready = sem("consts_ready")
        var_ready, std_ready, ln_ready = sem("var_ready"), sem("std_ready"), sem("ln_ready")
        lnT_psum, lnT_ready = sem("lnT_psum"), sem("lnT_ready")
        wqhi_ready, wqlo_ready, wkhi_ready, wklo_ready = sem("wqhi_ready"), sem("wqlo_ready"), sem("wkhi_ready"), sem("wklo_ready")
        lnT_lo_ready, q_psum, q_ready, qlo_ready = sem("lnT_lo_ready"), sem("q_psum"), sem("q_ready"), sem("qlo_ready")
        qk_psum, qk_ready = sem("qk_psum"), sem("qk_ready")
        late_hi, late_lo, cT_lo_ready = sem("late_hi"), sem("late_lo"), sem("cT_lo_ready")
        bkb_ready, qb_psum = sem("bkb_ready"), sem("qb_psum")
        hi1_ready, lo1_ready, s_psum = sem("hi1_ready"), sem("lo1_ready"), sem("s_psum")
        att_ready, max_done = sem("att_ready"), sem("max_done")
        maxT_psum, diag_ready, maxb_psum, shift_ready = sem("maxT_psum"), sem("diag_ready"), sem("maxb_psum"), sem("shift_ready")
        shifted, exp_done, p_hi_ready, p_lo_ready, summed = sem("shifted"), sem("exp_done"), sem("p_hi_ready"), sem("p_lo_ready"), sem("summed")
        hi2_ready, lo2_ready, pv_done = sem("hi2_ready"), sem("lo2_ready"), sem("pv_done")
        sum_psum, cT_even, cT_odd, o_psum = sem("sum_psum"), sem("cT_even"), sem("cT_odd"), sem("o_psum")
        sum_read = sem("sum_read")
        qkv_psum, qk2_ready, v_ready = sem("qkv_psum"), sem("qk2_ready"), sem("v_ready")
        sc_psum, nbias_ready, probs_ready, pT_psum, pT_ready, y_psum = sem("sc_psum"), sem("nbias_ready"), sem("probs_ready"), sem("pT_psum"), sem("pT_ready"), sem("y_psum")
        split3_ready, logit_psum, logit_ready, gexp_ready = sem("split3_ready"), sem("logit_psum"), sem("logit_ready"), sem("gexp_ready")
        taken_ready, place_psum, gate_ready, turned_psum, turned_ready = sem("taken_ready"), sem("place_psum"), sem("gate_ready"), sem("turned_psum"), sem("turned_ready")
        iota_ready, more_ready, wb_psum, wb_ready = sem("iota_ready"), sem("more_ready"), sem("wb_psum"), sem("wb_ready")
        t_hi_ready, t_lo_ready, pick_ready = sem("t_hi_ready"), sem("t_lo_ready"), sem("pick_ready")
        gather_hi_psum, gather_lo_psum, xg_hi_ready, xg_lo_ready = sem("gather_hi_psum"), sem("gather_lo_psum"), sem("xg_hi_ready"), sem("xg_lo_ready")
        place_b_psum, back_ready, own_ready = sem("place_b_psum"), sem("back_ready"), sem("own_ready")
        y_hi_ready, y_lo_ready, scatter_psum, added = sem("y_hi_ready"), sem("y_lo_ready"), sem("scatter_psum"), sem("added")
        down_hi_ready, down_lo_ready = sem("down_hi_ready"), sem("down_lo_ready")
        whi_ready, wlo_ready, g_psum, u_psum = sem("whi_ready"), sem("wlo_ready"), sem("g_psum"), sem("u_psum")
        silu_done, prod_done, hhi_ready, h_ready, down_done = sem("silu_done"), sem("prod_done"), sem("hhi_ready"), sem("h_ready"), sem("down_done")

        def first_tile(e):
            return e * ET + SH

        block = scope.enter_context(nc.Block())

        @block.sync
        def _(sp):
            for st in range(ST):
                sp.dma_start(x[:, st, :], x_in[st * P:(st + 1) * P, :]).then_inc(x_loaded[st], 16)
            sp.dma_start(wq[:, :, :], wq_in).then_inc(wq_loaded, 16)
            sp.dma_start(wk[:, :, :], wk_in).then_inc(wk_loaded, 16)
            for s in range(U):
                sp.dma_start(ring1[:, s, :, :], stream1[s]).then_inc(ring1_full[s], 16)
            with sp.Fori(1, CT // U) as g:
                for s in range(U):
                    sp.wait_ge(att_ready, g * U + (s - U + 1 + SB))
                    sp.dma_start(ring1[:, s, :, :], stream1[g * U + s]).then_inc(ring1_full[s], 16)
            for s in range(R2):
                sp.dma_start(ring2[:, s, :, :], ctx_in[s]).then_inc(ring2_full[s], 16)

            def refill2(first, last):
                with sp.Fori(first, last) as g:
                    for s in range(R2):
                        sp.wait_ge(lo2_ready, g * R2 + (s - R2 + 1))
                        sp.dma_start(ring2[:, s, :, :], ctx_in[g * R2 + s]).then_inc(ring2_full[s], 16)

            refill2(1, 4)
            sp.wait_ge(exp_done, 6)
            sp.dma_start(wqkv[:, :, :], wqkv_in).then_inc(wqkv_loaded, 16)
            sp.wait_ge(exp_done, 8)
            sp.dma_start(wv[:, :, :], wv_in).then_inc(wv_loaded, 16)
            refill2(4, CT // 2 // R2)
            sp.wait_ge(late_lo, KC + 2)
            sp.wait_ge(sum_psum, 1)
            for n in range(SH):
                if n >= RAW:
                    sp.wait_ge(down_lo_ready, n - RAW + 1)
                sp.dma_start(raw[:, n % RAW, :, :], shared_in[n]).then_inc(raw_full[n % RAW], 16)

            def unit(e, expert_):
                for j in range(ET):
                    slot = (SH + j) % RAW
                    sp.wait_ge(down_lo_ready, e * ET + (SH + j - RAW + 1))
                    if j < ET - 1:
                        sp.dma_start(raw[:, slot, :, :], full_in[expert_ * (ET - 1) + j]).then_inc(raw_full[slot], 16)
                    else:
                        sp.dma_start(raw[:, slot, 0, :], half_up_in[expert_]).then_inc(raw_full[slot], 16)
                        sp.dma_start(raw[0:HALF, slot, 1, :], half_down_in[expert_]).then_inc(raw_full[slot], 16)

            with sp.Fori(0, E) as e:
                unit(e, e)
            sp.wait_ge(more_ready, 1)
            extra = sp.value_load(more[0:1, 0:1], min_val=0, max_val=MORE)
            for m in range(MORE):
                with sp.If(extra > m):
                    unit(E + m, sp.value_load(which[0:1, m:m + 1], min_val=0, max_val=E - 1))
            for st in range(ST):
                sp.wait_ge(added, extra * ST + (E * ST + st + 1))
                sp.dma_start(out[st * P:(st + 1) * P, :], x[:, st, :]).then_inc(out_stored, 16)
            sp.wait_ge(out_stored, 16 * ST)

        @block.gpsimd
        def _(pool):
            steps = [0]

            def step(ins):
                steps[0] += 1
                ins.then_inc(pool_step, 1)
                pool.wait_ge(pool_step, steps[0])

            step(pool.memset(ident[:, :], 0.0))
            step(pool.affine_select(out=ident[:, :], in_=ident[:, :], compare_op=ALU.not_equal, fill=1.0,
                                    base=0, pattern=[[-1, P]], channel_multiplier=1))
            step(pool.memset(ones[:, :], 1.0))
            step(pool.memset(causal[:, :], 0.0))
            step(pool.affine_select(out=causal[:, :], in_=causal[:, :], compare_op=ALU.is_ge, fill=NEG,
                                    base=0, pattern=[[-1, P]], channel_multiplier=1))
            step(pool.memset(lower[:, :], 1.0))
            low = lower[:, :].rearrange("p (e j) -> p e j", j=E)
            pool.affine_select(out=low, in_=low, compare_op=ALU.is_gt, fill=0.0,
                               base=0, pattern=[[1, E], [-1, E]], channel_multiplier=0).then_inc(consts_ready, 1)

            pool.wait_ge(wqhi_ready, 1)
            pool.tensor_tensor(wq_lo[:, 2:4, :], wq[:, 2:4, :], wq_hi[:, 2:4, :].bitcast(F32),
                               ALU.subtract).then_inc(wqlo_ready, 1)
            pool.wait_ge(wkhi_ready, 1)
            pool.tensor_tensor(wk_lo[:, :, :], wk[:, :, :], wk_hi[:, :, :].bitcast(F32), ALU.subtract).then_inc(wklo_ready, 1)
            with pool.Fori(0, CT // U) as g:
                for s in range(U):
                    pool.wait_ge(hi1_ready, g * U + (s + 1))
                    pool.tensor_tensor(c_lo[:, s % 2, :], ring1[:, s, 0, :], c_hi[:, s % 2, :].bitcast(F32),
                                       ALU.subtract).then_inc(lo1_ready, 1)
            pool.wait_ge(shifted, 1)
            with pool.Fori(1, CT // 2) as m:
                rows = att[:, bass.ds(m * 2, 2), :]
                pool.tensor_tensor(rows, rows, shift[:, :].unsqueeze(1).to_broadcast([P, 2, S]),
                                   ALU.add).then_inc(shifted, 1)
            for k in range(KC):
                pool.wait_ge(late_hi, k + 1)
                pool.tensor_tensor(wqkv_lo[:, k, :], wqkv[:, k, :], wqkv_hi[:, k, :].bitcast(F32),
                                   ALU.subtract).then_inc(late_lo, 1)
            for k in range(0, KC, 2):
                pool.wait_ge(late_hi, KC + k // 2 + 1)
                pool.tensor_tensor(wv_lo[:, k:k + 2, :], wv[:, k:k + 2, :], wv_hi[:, k:k + 2, :].bitcast(F32),
                                   ALU.subtract).then_inc(late_lo, 1)
            def low_parts(n, slot, w_slot_):
                pool.wait_ge(whi_ready, n + 1)
                pool.tensor_tensor(w_lo[:, w_slot_, 0:2, :], raw[:, slot, 0:2, :], w_hi[:, w_slot_, 0:2, :].bitcast(F32),
                                   ALU.subtract).then_inc(wlo_ready, 1)
                pool.wait_ge(down_hi_ready, n + 1)
                pool.tensor_tensor(w_lo[:, w_slot_, 2, :], raw[:, slot, 2, :], w_hi[:, w_slot_, 2, :].bitcast(F32),
                                   ALU.subtract).then_inc(down_lo_ready, 1)

            low_parts(0, 0, 0)
            pool.wait_ge(logit_psum, 1)
            pool.wait_ge(split3_ready, ST)
            pool.iota(slot_row[:, :], pattern=[[1, CAP]], base=0, channel_multiplier=0,
                      allow_small_or_imprecise_dtypes=True).then_inc(iota_ready, 1)
            pool.iota(slot_col[:, :], pattern=[[P, 2]], base=0, channel_multiplier=1,
                      allow_small_or_imprecise_dtypes=True).then_inc(iota_ready, 1)

            for n in range(1, SH):
                low_parts(n, n % RAW, n % HL)
            pool.wait_ge(more_ready, 1)
            with pool.Fori(0, pool.value_load(more[0:1, 0:1], min_val=0, max_val=MORE) + E) as e:
                for j in range(ET - 1):
                    low_parts(e * ET + (SH + j), (SH + j) % RAW, (SH + j) % HL)
                slot, w = (SH + ET - 1) % RAW, (SH + ET - 1) % HL
                pool.wait_ge(whi_ready, e * ET + (SH + ET))
                pool.tensor_tensor(w_lo[:, w, 0, :], raw[:, slot, 0, :], w_hi[:, w, 0, :].bitcast(F32),
                                   ALU.subtract).then_inc(wlo_ready, 1)
                pool.wait_ge(down_hi_ready, e * ET + (SH + ET))
                pool.tensor_tensor(w_lo[0:HALF, w, 1, :], raw[0:HALF, slot, 1, :],
                                   w_hi[0:HALF, w, 1, :].bitcast(F32), ALU.subtract).then_inc(down_lo_ready, 1)

        @block.scalar
        def _(act):
            act.dma_start(cols[:, 0:16], cols_in).then_inc(small_loaded, 16)
            act.dma_start(betas[:, :], betas_in.to_broadcast([P, 3])).then_inc(small_loaded, 16)
            act.dma_start(gate[:, :, :], gate_in).then_inc(small_loaded, 16)
            act.dma_start(bv_b[:, :], bv_in.to_broadcast([P, D])).then_inc(small_loaded, 16)

            def root(n, i, st):
                act.wait_ge(var_ready, (n - 1) * ST + i + 1)
                act.activation(std[:, st:st + 1], mv[:, st, 1:2], ACT.Sqrt).then_inc(std_ready, 1)

            def evacuate_lnT(n, i, st, to, bank):
                cut = slice(st * P, (st + 1) * P)
                act.wait_ge(lnT_psum, (n - 1) * ST + i + 1)
                turned = ps[:, bank + st, :].rearrange("p (k c) -> p k c", k=KC)
                act.activation(to[:, :, cut], turned, ACT.Copy).then_inc(lnT_ready, 1)

            for st in range(ST):
                root(1, st, st)
            act.wait_ge(wq_loaded, 16)
            act.activation(wq_hi[:, :, :], wq[:, :, :], ACT.Copy).then_inc(wqhi_ready, 1)
            evacuate_lnT(1, 0, 0, lna_hi, 4)
            evacuate_lnT(1, 1, 1, lna_hi, 4)
            act.wait_ge(wk_loaded, 16)
            act.activation(wk_hi[:, :, :], wk[:, :, :], ACT.Copy).then_inc(wkhi_ready, 1)
            evacuate_lnT(1, 2, 2, lna_hi, 4)
            evacuate_lnT(1, 3, 3, lna_hi, 4)
            act.wait_ge(small_loaded, 64)
            for e in range(KC):
                act.wait_ge(q_psum, e + 1)
                act.activation(q32[:, e, :], ps[:, e, :], ACT.Identity, bias=cols[:, e:e + 1]).then_inc(q_ready, 1)
            with act.Fori(0, CT // U) as g:
                for s in range(U):
                    act.wait_ge(s_psum, g * U + (s + 1))
                    act.wait_ge(ring1_full[s], g * 16 + 16)
                    act.activation(c_hi[:, s % 2, :], ring1[:, s, 0, :], ACT.Copy).then_inc(hi1_ready, 1)
            act.wait_ge(s_psum, CT + 2)
            def pair(g, s):
                act.wait_ge(summed, g * R2 + (s + 1))
                act.wait_ge(shifted, g * R2 + (s + 1))
                act.activation(p32[:, s % 2, :, :], att[:, bass.ds((g * R2 + s) * 2, 2), :],
                               ACT.Exp).then_inc(exp_done, 1)
                act.wait_ge(pv_done, g * R2 + (s + 1))
                act.wait_ge(ring2_full[s], g * 16 + 16)
                act.activation(d_hi[:, s % 2, :, :], ring2[:, s, :, :], ACT.Copy).then_inc(hi2_ready, 1)
                act.wait_ge(exp_done, g * R2 + (s + 1))
                act.activation(p_hi[:, s % 2, :, :], p32[:, s % 2, :, :], ACT.Copy).then_inc(p_hi_ready, 1)

            with act.Fori(0, CT // 2 // R2 - 2) as g:
                for s in range(R2):
                    pair(g, s)
            act.wait_ge(wqkv_loaded, 16)
            act.wait_ge(wv_loaded, 16)
            for n in range(2 * R2):
                pair(CT // 2 // R2 - 2 + n // R2, n % R2)
                if n < KC:
                    act.activation(wqkv_hi[:, n, :], wqkv[:, n, :], ACT.Copy).then_inc(late_hi, 1)
                elif n < KC + 2:
                    k = 2 * (n - KC)
                    act.activation(wv_hi[:, k:k + 2, :], wv[:, k:k + 2, :], ACT.Copy).then_inc(late_hi, 1)

            act.wait_ge(pv_done, CT // 2 + 2)
            act.dma_start(bqkv_b[:, :], bqkv_in.to_broadcast([P, D])).then_inc(bqkv_loaded, 16)
            for k in range(0, KC, 2):
                act.activation(cT_hi[:, k, :], ps[:, 4 + k, :], ACT.Copy).then_inc(cT_even, 1)
            root(2, 0, 0)
            root(2, 1, 1)
            root(2, 2, 2)
            evacuate_lnT(2, 0, 0, lnT_hi, 4)
            root(2, 3, 3)
            for st in range(1, ST):
                evacuate_lnT(2, st, st, lnT_hi, 4)
            for j in range(2 * KC):
                act.wait_ge(qkv_psum, ST + j + 1)
                to = (qT if j < KC else kT)[:, j % KC, :]
                act.activation(to, ps[:, (4 + j) % 8, :], ACT.Identity, bias=cols[:, 8 + j:9 + j]).then_inc(qk2_ready, 1)

            def exponentials(n, i):
                w = (i + 1) * P
                act.wait_ge(nbias_ready, n + 1)
                act.activation(probs[:, i, 0:w], ps[:, 4 + i, 0:w], ACT.Exp, bias=nbias[:, i:i + 1], scale=SCALE,
                               accum_out=rowsum[:, i:i + 1]).then_inc(probs_ready, 1)

            def evacuate_pT(n, i):
                w = (i + 1) * P
                act.wait_ge(pT_psum, n + 1)
                act.activation(pT[:, i, 0:w], ps[:, i, 0:w], ACT.Copy).then_inc(pT_ready, 1)

            for n, i in enumerate(DOWN):
                exponentials(n, i)
                if n >= 1:
                    evacuate_pT(n - 1, DOWN[n - 1])
            evacuate_pT(ST - 1, DOWN[ST - 1])

            def high_parts(n, k, fill, half=False):
                slot, w = k % RAW, k % HL
                act.wait_ge(down_done, n + (1 - HL + CREDIT))
                act.wait_ge(raw_full[slot], fill)
                if half:
                    act.activation(w_hi[:, w, 0, :], raw[:, slot, 0, :], ACT.Copy).then_inc(whi_ready, 1)
                    act.activation(w_hi[0:HALF, w, 1, :], raw[0:HALF, slot, 1, :], ACT.Copy).then_inc(down_hi_ready, 1)
                else:
                    act.activation(w_hi[:, w, 0:2, :], raw[:, slot, 0:2, :], ACT.Copy).then_inc(whi_ready, 1)
                    act.activation(w_hi[:, w, 2, :], raw[:, slot, 2, :], ACT.Copy).then_inc(down_hi_ready, 1)

            def shared_high(n):
                if n < SH:
                    high_parts(n, n, 16 * (n // RAW + 1))

            def expert_high(e, j):
                e, j = (e + 1 if j >= ET else e), j % ET
                shared = len([n for n in range(SH) if n % RAW == (SH + j) % RAW])
                half = j == ET - 1
                high_parts(e * ET + (SH + j), SH + j, (e * 32 + (shared * 16 + 32)) if half else (e * 16 + (shared * 16 + 16)), half)

            def silu(n, k, width, half=False):
                act.wait_ge(g_psum, n + 1)
                act.wait_ge(prod_done, n + (1 - 2 + CREDIT))
                p = k % 2
                if half:
                    act.activation(up_half[:, :], ps[HALF:2 * HALF, p, 0:width], ACT.Copy)
                    act.activation(gated[0:HALF, p, 0:width], ps[0:HALF, p, 0:width], ACT.Silu).then_inc(silu_done, 1)
                else:
                    act.activation(gated[:, p, 0:width], ps[:, p, 0:width], ACT.Silu).then_inc(silu_done, 1)

            def gathered(e, banks):
                act.wait_ge(gather_hi_psum, e + 1)
                act.activation(xg_hi[:, :, :].rearrange("p k c -> p (k c)"),
                               ps[:, banks:banks + 2, :].rearrange("p a b -> p (a b)"), ACT.Copy).then_inc(xg_hi_ready, 1)

            def output(e):
                act.wait_ge(down_done, e * ET + (SH + ET + CREDIT))
                act.activation(y_hi[:, :, :], ps[:, 2:4, :], ACT.Copy).then_inc(y_hi_ready, 1)

            def unit(e, first=False, last=False):
                for j in range(ET):
                    if j == 0 and not first:
                        output(e - 1)
                    silu(e * ET + (SH + j), SH + j, CAP, j == ET - 1)
                    if j == ET - 1 and not last:
                        gathered(e + 1, 4)
                    if not (last and j + 2 >= ET):
                        expert_high(e, j + 2)
                if last:
                    output(e)

            for n, st in enumerate(DOWN):
                root(3, n, st)
            act.wait_ge(y_psum, ST)
            shared_high(0)
            for n, st in enumerate(DOWN):
                evacuate_lnT(3, n, st, ln3T, 0)
            shared_high(1)
            act.wait_ge(logit_ready, 1)
            act.activation(ex[:, :, 0:E], lg[:, :, 0:E], ACT.Exp).then_inc(gexp_ready, 1)
            act.activation(ex[:, :, E], lg[:, :, E], ACT.Exp, scale=-1.0).then_inc(gexp_ready, 1)
            act.activation(t_hi[:, :, :], ln[:, :, :], ACT.Copy).then_inc(t_hi_ready, 1)
            for n in range(SH):
                silu(n, n, S)
                if n == 0:
                    act.wait_ge(wb_psum, 1)
                    act.activation(wb[:, :], ps[:, 7, :], ACT.Copy).then_inc(wb_ready, 1)
                if n + 2 < SH:
                    shared_high(n + 2)
                else:
                    expert_high(0, n + 2 - SH)
            gathered(0, 0)
            unit(0, first=True)
            act.wait_ge(more_ready, 1)
            final = act.value_load(more[0:1, 0:1], min_val=0, max_val=MORE) + (E - 1)
            with act.Fori(1, final) as e:
                unit(e)
            unit(final, last=True)

        @block.tensor
        def _(pe):
            pe.sem_inc(s_psum, 2)
            pe.sem_inc(pv_done, 2)
            pe.sem_inc(down_done, CREDIT)

            def turn_ln(n, i, st, src, bank):
                pe.wait_ge(ln_ready, (n - 1) * ST + i + 1)
                for k in range(KC):
                    mm = pe.transpose(ps[:, bank + st, k * P:(k + 1) * P], src[:, st, k * P:(k + 1) * P],
                                      ident[:, :])
                mm.then_inc(lnT_psum, 1)

            def product(bank, width, lhs, rhs, terms):
                for k in range(terms):
                    mm = pe.matmul(ps[:, bank, 0:width], lhs(k), rhs(k), start=(k == 0), stop=(k == terms - 1))
                return mm

            def split_product(bank, width, lhs, rhs, terms, term_ready=None):
                for k in range(terms):
                    if term_ready is not None:
                        pe.wait_ge(term_ready, k + 1)
                    (lh, ll), (rh, rl) = lhs(k), rhs(k)
                    pe.matmul(ps[:, bank, 0:width], lh, rh, start=(k == 0), stop=False)
                    pe.matmul(ps[:, bank, 0:width], lh, rl, start=False, stop=False)
                    mm = pe.matmul(ps[:, bank, 0:width], ll, rh, start=False, stop=(k == terms - 1))
                return mm

            def both(hi, lo, k, a, b):
                return hi[:, k, a:b], lo[:, k, a:b]

            def open_sums():
                for b in range(4, 8):
                    for q in range(4):
                        pe.matmul(ps[:, b, q * P:(q + 1) * P], zero16[:, :], zero16[:, :], start=(q == 0), stop=False,
                                  skip_group_check=True)

            pe.wait_ge(consts_ready, 1)
            for st in range(ST):
                turn_ln(1, st, st, ln_a, 4)
            pe.wait_ge(lnT_ready, ST)
            pe.wait_ge(lnT_lo_ready, ST)
            pe.wait_ge(wqlo_ready, 2)
            for e in range(KC):
                split_product(e, S, lambda k: both(wq_hi, wq_lo, k, e * P, (e + 1) * P),
                              lambda k: both(lna_hi, lna_lo, k, 0, S), KC).then_inc(q_psum, 1)
            pe.wait_ge(wklo_ready, 1)
            for d in range(KC):
                split_product(4 + d, S, lambda k: both(wk_hi, wk_lo, k, d * P, (d + 1) * P),
                              lambda k: both(q_hi, q_lo, k, 0, S), KC,
                              term_ready=qlo_ready).then_inc(qk_psum, 1)
            pe.wait_ge(bkb_ready, 1)
            split_product(3, S, lambda k: both(bkb_hi, bkb_lo, k, 0, P),
                          lambda k: both(q_hi, q_lo, k, 0, S), KC).then_inc(qb_psum, 1)
            pe.wait_ge(qk_ready, KC + 1)

            with pe.Fori(0, CT // U) as g:
                for s in range(U):
                    pe.wait_ge(hi1_ready, g * U + (s + 1))
                    pe.wait_ge(att_ready, g * U + (s + 1))
                    for k in range(KC):
                        hi = c_hi[:, s % 2, k * P:(k + 1) * P]
                        pe.matmul(ps[:, s, :], hi, qk_hi[:, k, :], start=(k == 0), stop=False)
                        pe.matmul(ps[:, s, :], hi, qk_lo[:, k, :], start=False, stop=False)
                    pe.wait_ge(lo1_ready, g * U + (s + 1))
                    for k in range(KC):
                        mm = pe.matmul(ps[:, s, :], c_lo[:, s % 2, k * P:(k + 1) * P], qk_hi[:, k, :],
                                       start=False, stop=(k == KC - 1))
                    mm.then_inc(s_psum, 1)
            pe.wait_ge(max_done, CT + 1)
            for q in range(ST):
                mm = pe.transpose(ps[:, 0, q * P:(q + 1) * P], runmax[:, q * P:(q + 1) * P], ident[:, :])
            mm.then_inc(maxT_psum, 1)
            pe.wait_ge(diag_ready, 1)
            for q in range(ST):
                mm = pe.matmul(ps[:, 1, q * P:(q + 1) * P], ones[:, :], diag[:, q, :], start=True, stop=True)
            mm.then_inc(maxb_psum, 1)

            open_sums()
            with pe.Fori(0, CT // 2 // R2) as g:
                for s in range(R2):
                    m = g * R2 + (s + 1)
                    slot = s % 2

                    def add(a, b):
                        for t in range(2):
                            for d in range(KC):
                                mm = pe.matmul(ps[:, 4 + d, :], a[:, slot, t, d * P:(d + 1) * P], b[:, slot, t, :],
                                               start=False, stop=False, skip_group_check=True)
                        return mm

                    pe.wait_ge(hi2_ready, m)
                    pe.wait_ge(p_hi_ready, m)
                    add(d_hi, p_hi)
                    pe.wait_ge(lo2_ready, m)
                    add(d_lo, p_hi)
                    pe.wait_ge(p_lo_ready, m)
                    add(d_hi, p_lo).then_inc(pv_done, 1)
            pe.wait_ge(summed, CT // 2 + 2)
            for st in range(ST):
                for t in range(2):
                    mm = pe.matmul(ps[:, 3, st:st + 1], expsum[:, t, st * P:(st + 1) * P], ones[:, 0:1],
                                   start=(t == 0), stop=(t == 1))
            mm.then_inc(sum_psum, 1)
            pe.wait_ge(late_lo, KC + 2)
            pe.wait_ge(cT_even, KC // 2)
            pe.wait_ge(cT_odd, KC // 2)

            def out_high(st):
                for k in range(KC):
                    a = cT_hi[:, k, st * P:(st + 1) * P]
                    pe.matmul(ps[:, st, :], a, wv_hi[:, k, :], start=(k == 0), stop=False)
                    pe.matmul(ps[:, st, :], a, wv_lo[:, k, :], start=False, stop=False)

            def out_low(st):
                pe.wait_ge(cT_lo_ready, KC)
                for k in range(KC):
                    mm = pe.matmul(ps[:, st, :], cT_lo[:, k, st * P:(st + 1) * P], wv_hi[:, k, :],
                                   start=False, stop=(k == KC - 1))
                mm.then_inc(o_psum, 1)

            out_high(0)
            for st in range(ST):
                if st + 1 < ST:
                    if st + 1 == ST - 1:
                        pe.wait_ge(sum_read, 1)
                    out_high(st + 1)
                out_low(st)

            def value(st):
                pe.wait_ge(lnT_ready, ST + st + 1)
                pe.wait_ge(lnT_lo_ready, ST + st + 1)
                split_product(st, D, lambda k: both(lnT_hi, lnT_lo, k, st * P, (st + 1) * P),
                              lambda k: both(wqkv_hi, wqkv_lo, k, 2 * D, 3 * D), KC).then_inc(qkv_psum, 1)

            for st in range(ST):
                turn_ln(2, st, st, ln, 4)
                if st >= 1:
                    value(st - 1)
            value(ST - 1)
            for j in range(2 * KC):
                if j >= KC:
                    pe.wait_ge(v_ready, j - KC + 1)
                split_product((4 + j) % 8, S, lambda k: both(wqkv_hi, wqkv_lo, k, j * P, (j + 1) * P),
                              lambda k: both(lnT_hi, lnT_lo, k, 0, S), KC).then_inc(qkv_psum, 1)
            pe.wait_ge(qk2_ready, 2 * KC)
            for i in DOWN:
                w = (i + 1) * P
                product(4 + i, w, lambda k: qT[:, k, i * P:(i + 1) * P], lambda k: kT[:, k, 0:w], KC).then_inc(sc_psum, 1)

            def turn_probs(n, i):
                pe.wait_ge(probs_ready, n + 1)
                for k in range(i + 1):
                    mm = pe.transpose(ps[:, i, k * P:(k + 1) * P], probs[:, i, k * P:(k + 1) * P], ident[:, :])
                mm.then_inc(pT_psum, 1)

            def attend(n, i):
                pe.wait_ge(pT_ready, n + 1)
                product(4 + i, D, lambda k: pT[:, i, k * P:(k + 1) * P], lambda k: v[:, k, :], i + 1).then_inc(y_psum, 1)

            for n, i in enumerate(DOWN):
                turn_probs(n, i)
                if n >= 1:
                    attend(n - 1, DOWN[n - 1])
            attend(ST - 1, DOWN[ST - 1])

            for n, st in enumerate(DOWN):
                turn_ln(3, n, st, ln, 0)
            for n, st in enumerate(DOWN):
                pe.wait_ge(lnT_ready, 2 * ST + n + 1)
                for k in range(KC):
                    mm = pe.matmul(ps[:, 4, 16 * st:16 * st + E + 1], ln3T[:, k, st * P:(st + 1) * P], gate[:, k, :],
                                   start=(k == 0), stop=(k == KC - 1))
            mm.then_inc(logit_psum, 1)

            def wait_split(n):
                pe.wait_ge(whi_ready, n + 1)
                pe.wait_ge(wlo_ready, n + 1)
                pe.wait_ge(prod_done, n + (1 - 2 + CREDIT))

            def up_shared(n):
                wait_split(n)
                for part, bank, done in ((0, n % 2, g_psum), (1, 2 + n % 2, u_psum)):
                    split_product(bank, S, lambda k: tuple(w[:, n % HL, part, k * P:(k + 1) * P] for w in (w_hi, w_lo)),
                                  lambda k: both(l_hi, l_lo, k, 0, S), KC).then_inc(done, 1)

            def down_shared(n):
                pe.wait_ge(h_ready, n + 1)
                pe.wait_ge(down_hi_ready, n + 1)
                pe.wait_ge(down_lo_ready, n + 1)
                for st in range(ST):
                    hi, lo = (h[:, n % 2, st * P:(st + 1) * P] for h in (h_hi, h_lo))
                    for a, b in ((hi, w_hi), (hi, w_lo), (lo, w_hi)):
                        mm = pe.matmul(ps[:, 4 + st, :], a, b[:, n % HL, 2, :], start=False, stop=(n == SH - 1),
                                       skip_group_check=True)
                mm.then_inc(down_done, 1)

            def up(e, j):
                k = SH + j
                wait_split(e * ET + k)
                for part in range(1 if j == ET - 1 else 2):
                    out_ = ps[:, k % 2, part * CAP:(part + 1) * CAP]
                    for c in range(KC):
                        hi, lo = (w[:, k % HL, part, c * P:(c + 1) * P] for w in (w_hi, w_lo))
                        pe.matmul(out_, hi, xg_hi[:, c, :], start=(c == 0), stop=False)
                        pe.matmul(out_, hi, xg_lo[:, c, :], start=False, stop=False)
                        mm = pe.matmul(out_, lo, xg_hi[:, c, :], start=False, stop=(c == KC - 1))
                mm.then_inc(g_psum, 1)

            def down(e, j):
                k = SH + j
                rows_ = HALF if j == ET - 1 else P
                part = 1 if j == ET - 1 else 2
                pe.wait_ge(h_ready, e * ET + (k + 1))
                pe.wait_ge(down_hi_ready, e * ET + (k + 1))
                pe.wait_ge(down_lo_ready, e * ET + (k + 1))
                for s in range(2):
                    hi, lo = (h[0:rows_, k % 2, s * P:(s + 1) * P] for h in (h_hi, h_lo))
                    for t, (a, b) in enumerate(((hi, w_hi), (hi, w_lo), (lo, w_hi))):
                        mm = pe.matmul(ps[:, 2 + s, :], a, b[0:rows_, k % HL, part, :], start=(j == 0 and t == 0),
                                       stop=(j == ET - 1 and t == 2))
                mm.then_inc(down_done, 1)

            def gather(e, banks):
                for part, bank, done in ((t_hi, banks, gather_hi_psum), (t_lo, banks + 2, gather_lo_psum)):
                    for k in range(KC):
                        for st in range(ST):
                            mm = pe.matmul(ps[:, bank + k // 2, (k % 2) * CAP:(k % 2 + 1) * CAP],
                                           part[:, st, k * P:(k + 1) * P],
                                           pick[:, bass.ds(e * ST + st, 1), :].rearrange("p a c -> p (a c)"),
                                           start=(st == 0), stop=(st == ST - 1))
                    mm.then_inc(done, 1)

            def spread_place(e):
                pe.wait_ge(own_ready, e + 1)
                pe.matmul(ps[:, 4, :], ones_r[0:NU, :], own_places[0:NU, :], start=True,
                          stop=True).then_inc(place_b_psum, 1)

            def scatter(e, first_st, last_st):
                pe.wait_ge(back_ready, e + 1)
                pe.wait_ge(y_hi_ready, e + 1)
                pe.wait_ge(y_lo_ready, e + 1)
                for st in range(first_st, last_st):
                    for s in range(2):
                        for part in (y_hi, y_lo):
                            mm = pe.matmul(ps[:, 4 + st, :], back[:, s, st * P:(st + 1) * P], part[:, s, :],
                                           start=(s == 0 and part is y_hi), stop=(s == 1 and part is y_lo))
                    mm.then_inc(scatter_psum, 1)

            def turn_places():
                pe.wait_ge(added, ST)
                for st in range(ST):
                    mm = pe.matmul(ps[0:NU, 4, st * P:(st + 1) * P], place[:, st, :], ident[:, :],
                                   start=True, stop=True)
                mm.then_inc(turned_psum, 1)

            def unit(e, first=False, last=False):
                pe.wait_ge(xg_hi_ready, e + 1)
                pe.wait_ge(xg_lo_ready, e + 1)
                if first:
                    turn_places()
                else:
                    spread_place(e - 1)
                up(e, 0)
                up(e, 1)
                if not first:
                    scatter(e - 1, 0, ST // 2)
                down(e, 0)
                if not first:
                    scatter(e - 1, ST // 2, ST)
                for j in range(2, ET):
                    up(e, j)
                    if j == ET - 1 and not last:
                        if first:
                            pe.wait_ge(turned_ready, 1)
                        pe.wait_ge(added, (e + 1) * ST)
                        gather(e + 1, 4)
                    down(e, j - 1)
                down(e, ET - 1)
                if last:
                    spread_place(e)
                    scatter(e, 0, ST)

            pe.wait_ge(split3_ready, KC)
            up_shared(0)
            pe.wait_ge(taken_ready, 1)
            for st in range(ST):
                for q in range(st + 1):
                    pe.matmul(ps[:, 5, st * E:(st + 1) * E], before[:, :] if q == st else ones[:, :], taken[:, q, :],
                              start=(q == 0), stop=(q == st))
            for q in range(ST):
                mm = pe.matmul(ps[:, 5, ST * E:(ST + 1) * E], ones[:, :], taken[:, q, :],
                               start=(q == 0), stop=(q == ST - 1))
            mm.then_inc(place_psum, 1)
            pe.wait_ge(gate_ready, 1)
            pe.matmul(ps[:, 7, :], ones[:, :], gate_diag[:, :, :].rearrange("p t c -> p (t c)"), start=True,
                      stop=True).then_inc(wb_psum, 1)
            up_shared(1)
            pe.wait_ge(wb_ready, 1)
            pe.wait_ge(more_ready, 1)
            open_sums()
            for n in range(SH):
                if 1 <= n < SH - 1:
                    up_shared(n + 1)
                down_shared(n)
            pe.wait_ge(prod_done, SH + CREDIT)
            pe.wait_ge(pick_ready, 1)
            gather(0, 0)
            unit(0, first=True)
            final = pe.value_load(more[0:1, 0:1], min_val=0, max_val=MORE) + (E - 1)
            with pe.Fori(1, final) as e:
                unit(e)
            unit(final, last=True)

        @block.vector
        def _(dve):
            steps = [0]

            def step(ins):
                steps[0] += 1
                ins.then_inc(dve_step, 1)
                dve.wait_ge(dve_step, steps[0])

            def moments(st):
                step(dve.bn_stats(stats[:, st, :], x[:, st, :]))
                step(dve.bn_aggr(mv[:, st, :], stats[:, st, :]))
                dve.tensor_scalar(mv[:, st, 1:2], mv[:, st, 1:2], EPS, None, ALU.add).then_inc(var_ready, 1)

            def normalize(n, i, st, to):
                dve.wait_ge(std_ready, (n - 1) * ST + i + 1)
                step(dve.reciprocal(rstd[:, st:st + 1], std[:, st:st + 1]))
                dve.tensor_scalar(to[:, st, :], x[:, st, :], mv[:, st, 0:1], rstd[:, st:st + 1],
                                  ALU.subtract, ALU.mult).then_inc(ln_ready, 1)

            dve.sem_inc(att_ready, SB)
            dve.sem_inc(summed, 2)
            dve.sem_inc(prod_done, CREDIT)
            def low_lnT(n, i, st, hi, lo, bank):
                cut = slice(st * P, (st + 1) * P)
                dve.wait_ge(lnT_ready, (n - 1) * ST + i + 1)
                turned = ps[:, bank + st, :].rearrange("p (k c) -> p k c", k=KC)
                dve.tensor_tensor(lo[:, :, cut], turned, hi[:, :, cut].bitcast(F32),
                                  ALU.subtract).then_inc(lnT_lo_ready, 1)

            for st in range(ST):
                dve.wait_ge(x_loaded[st], 16)
                moments(st)
                if st >= 1:
                    normalize(1, st - 1, st - 1, ln_a)
            normalize(1, ST - 1, ST - 1, ln_a)
            dve.wait_ge(wqhi_ready, 1)
            dve.tensor_tensor(wq_lo[:, 0:2, :], wq[:, 0:2, :], wq_hi[:, 0:2, :].bitcast(F32),
                              ALU.subtract).then_inc(wqlo_ready, 1)
            for st in range(ST):
                low_lnT(1, st, st, lna_hi, lna_lo, 4)
            dve.wait_ge(consts_ready, 1)
            dve.wait_ge(small_loaded, 64)
            for k in range(KC):
                ins = dve.tensor_scalar(bkb[:, k, :], ones[:, :], cols[:, 4 + k:5 + k], None, ALU.mult)
            step(ins)
            step(dve.tensor_copy(bkb_hi[:, :, :], bkb[:, :, :]))
            dve.tensor_tensor(bkb_lo[:, :, :], bkb[:, :, :], bkb_hi[:, :, :].bitcast(F32), ALU.subtract).then_inc(bkb_ready, 1)
            dve.wait_ge(ln_ready, ST)
            for st in range(ST):
                ins = dve.tensor_tensor(x[:, st, :], x[:, st, :], bv_b[:, :], ALU.add)
            step(ins)
            step(dve.tensor_tensor(beta[:, :], betas[:, 0:1], betas[:, 1:2], ALU.add))
            step(dve.tensor_tensor(beta[:, :], beta[:, :], betas[:, 2:3], ALU.subtract))
            dve.memset(zero16[:, :], 0.0)
            dve.memset(runmax[:, :], -3.0e38).then_inc(max_done, 1)
            for e in range(KC):
                dve.wait_ge(q_ready, e + 1)
                step(dve.tensor_copy(q_hi[:, e, :], q32[:, e, :]))
                dve.tensor_tensor(q_lo[:, e, :], q32[:, e, :], q_hi[:, e, :].bitcast(F32),
                                  ALU.subtract).then_inc(qlo_ready, 1)
            for d in range(KC):
                dve.wait_ge(qk_psum, d + 1)
                step(dve.tensor_scalar(qk32[:, d, :], ps[:, 4 + d, :], SCALE, None, ALU.mult))
                step(dve.tensor_copy(qk_hi[:, d, :], qk32[:, d, :]))
                dve.tensor_tensor(qk_lo[:, d, :], qk32[:, d, :], qk_hi[:, d, :].bitcast(F32),
                                  ALU.subtract).then_inc(qk_ready, 1)
            dve.wait_ge(qb_psum, 1)
            dve.tensor_scalar(qb[:, :], ps[:, 3, :], SCALE, None, ALU.mult).then_inc(qk_ready, 1)

            with dve.Fori(0, CT // U) as g:
                for s in range(U):
                    dve.wait_ge(s_psum, g * U + (s + 1 + 2))
                    dve.scalar_tensor_tensor(out=att[:, g * U + s, :], in0=ring1[:, s, 1, :], scalar=beta[:, 0:1],
                                             in1=ps[:, s, :], op0=ALU.mult, op1=ALU.add).then_inc(att_ready, 1)
                    dve.wait_ge(att_ready, g * U + (s + 1 + SB))
                    dve.wait_ge(max_done, g * U + (s + 1))
                    dve.tensor_tensor(runmax[:, :], runmax[:, :], att[:, g * U + s, :], ALU.max).then_inc(max_done, 1)
            dve.wait_ge(maxT_psum, 1)
            step(dve.tensor_reduce(mcol[:, :], ps[:, 0, :].rearrange("p (q c) -> p q c", q=ST), AX_X, ALU.max))
            for q in range(ST):
                ins = dve.tensor_scalar(diag[:, q, :], ident[:, :], mcol[:, q:q + 1], None, ALU.mult)
            ins.then_inc(diag_ready, 1)
            dve.wait_ge(maxb_psum, 1)
            step(dve.tensor_tensor(shift_t[:, :], ps[:, 1, :], qb[:, :], ALU.add))
            dve.tensor_tensor(shift[:, :], qb[:, :], shift_t[:, :], ALU.subtract).then_inc(shift_ready, 1)
            dve.wait_ge(shift_ready, 1)
            dve.tensor_tensor(att[:, 0:2, :], att[:, 0:2, :], shift[:, :].unsqueeze(1).to_broadcast([P, 2, S]),
                              ALU.add).then_inc(shifted, 1)
            step(dve.memset(expsum[:, :, :], 0.0))
            with dve.Fori(0, CT // 2 // R2) as g:
                for s in range(R2):
                    m = g * R2 + (s + 1)
                    slot = s % 2
                    dve.wait_ge(hi2_ready, m)
                    dve.tensor_tensor(d_lo[:, slot, :, :], ring2[:, s, :, :], d_hi[:, slot, :, :].bitcast(F32),
                                      ALU.subtract).then_inc(lo2_ready, 1)
                    dve.wait_ge(p_hi_ready, m)
                    dve.tensor_tensor(p_lo[:, slot, :, :], p32[:, slot, :, :], p_hi[:, slot, :, :].bitcast(F32),
                                      ALU.subtract).then_inc(p_lo_ready, 1)
                    dve.wait_ge(summed, g * R2 + (s + 2))
                    dve.tensor_tensor(expsum[:, :, :], expsum[:, :, :], p32[:, slot, :, :], ALU.add).then_inc(summed, 1)
            dve.wait_ge(pv_done, CT // 2 + 2)
            for k in range(1, KC, 2):
                dve.tensor_copy(cT_hi[:, k, :], ps[:, 4 + k, :]).then_inc(cT_odd, 1)
            dve.wait_ge(cT_even, KC // 2)
            dve.wait_ge(cT_odd, KC // 2)
            for k in range(KC):
                dve.tensor_tensor(cT_lo[:, k, :], ps[:, 4 + k, :], cT_hi[:, k, :].bitcast(F32),
                                  ALU.subtract).then_inc(cT_lo_ready, 1)
            dve.wait_ge(sum_psum, 1)
            dve.reciprocal(rinv[:, :], ps[:, 3, 0:ST]).then_inc(sum_read, 1)
            dve.wait_ge(sum_read, 1)
            for st in range(ST):
                dve.wait_ge(o_psum, st + 1)
                step(dve.scalar_tensor_tensor(out=x[:, st, :], in0=ps[:, st, :], scalar=rinv[:, st:st + 1],
                                              in1=x[:, st, :], op0=ALU.mult, op1=ALU.add))
                moments(st)
                if st >= 1:
                    normalize(2, st - 1, st - 1, ln)
                if st >= 2:
                    low_lnT(2, st - 2, st - 2, lnT_hi, lnT_lo, 4)
            normalize(2, ST - 1, ST - 1, ln)
            low_lnT(2, ST - 2, ST - 2, lnT_hi, lnT_lo, 4)
            low_lnT(2, ST - 1, ST - 1, lnT_hi, lnT_lo, 4)

            dve.wait_ge(bqkv_loaded, 16)
            for st in range(ST):
                dve.wait_ge(qkv_psum, st + 1)
                dve.tensor_tensor(v[:, st, :], ps[:, st, :], bqkv_b[:, :], ALU.add).then_inc(v_ready, 1)
            for n, i in enumerate(DOWN):
                w = (i + 1) * P
                dve.wait_ge(sc_psum, n + 1)
                step(dve.tensor_tensor(ps[:, 4 + i, i * P:w], ps[:, 4 + i, i * P:w], causal[:, :], ALU.add))
                step(dve.tensor_reduce(mcol[:, i:i + 1], ps[:, 4 + i, 0:w], AX_X, ALU.max))
                dve.tensor_scalar(nbias[:, i:i + 1], mcol[:, i:i + 1], -SCALE, None, ALU.mult).then_inc(nbias_ready, 1)
            for n, i in enumerate(DOWN):
                dve.wait_ge(probs_ready, n + 1)
                step(dve.reciprocal(rinv[:, i:i + 1], rowsum[:, i:i + 1]))
                dve.wait_ge(y_psum, n + 1)
                step(dve.scalar_tensor_tensor(out=x[:, i, :], in0=ps[:, 4 + i, :], scalar=rinv[:, i:i + 1],
                                              in1=x[:, i, :], op0=ALU.mult, op1=ALU.add))
                moments(i)
                if n >= 1:
                    normalize(3, n - 1, DOWN[n - 1], ln)
            normalize(3, ST - 1, DOWN[ST - 1], ln)

            for n, st in enumerate(DOWN):
                cut = slice(st * P, (st + 1) * P)
                dve.wait_ge(lnT_ready, 2 * ST + n + 1)
                step(dve.tensor_copy(l_hi[:, :, cut], ln3T[:, :, cut]))
                dve.tensor_tensor(l_lo[:, :, cut], ln3T[:, :, cut], l_hi[:, :, cut].bitcast(F32),
                                  ALU.subtract).then_inc(split3_ready, 1)
            dve.wait_ge(logit_psum, 1)
            step(dve.tensor_copy(lg[:, :, :], ps[:, 4, 0:16 * ST].rearrange("p (t c) -> p t c", c=16)[:, :, 0:E + 1]))
            le = lg[:, :, 0:E]
            step(dve.tensor_reduce(mcol[:, :], le, AX_X, ALU.max))
            step(dve.tensor_tensor(le, le, mcol[:, :].unsqueeze(2).to_broadcast([P, ST, E]), ALU.subtract))
            dve.sem_inc(logit_ready, 1)
            other = le.unsqueeze(2).to_broadcast([P, ST, E, E])
            own = le.unsqueeze(3).to_broadcast([P, ST, E, E])
            gt = cmp_gt[:, :, :].rearrange("p t (e j) -> p t e j", j=E)
            ge = cmp_ge[:, :, :].rearrange("p t (e j) -> p t e j", j=E)
            dve.tensor_tensor(gt, other, own, ALU.is_gt)
            step(dve.tensor_tensor(ge, other, own, ALU.is_ge))
            step(dve.tensor_tensor(cmp_ge[:, :, :], cmp_ge[:, :, :],
                                   lower[:, :].unsqueeze(1).to_broadcast([P, ST, E * E]), ALU.mult))
            step(dve.tensor_tensor(cmp_gt[:, :, :], cmp_gt[:, :, :], cmp_ge[:, :, :], ALU.max))
            step(dve.tensor_reduce(rank[:, :, :], gt, AX_X, ALU.add))
            dve.tensor_scalar(before[:, :], causal[:, :], -1.0, None, ALU.is_lt)
            step(dve.tensor_scalar(taken[:, :, :], rank[:, :, :], 2.0, None, ALU.is_lt))
            dve.sem_inc(taken_ready, 1)
            dve.wait_ge(gexp_ready, 2)
            step(dve.tensor_reduce(rowsum[:, :], ex[:, :, 0:E], AX_X, ALU.add))
            step(dve.reciprocal(rinv[:, :], rowsum[:, :]))
            step(dve.tensor_scalar(ex[:, :, E], ex[:, :, E], 1.0, None, ALU.add))
            step(dve.reciprocal(gate_col[:, :], ex[:, :, E]))
            dve.tensor_tensor(gate_diag[:, :, :], ident[:, :].unsqueeze(1).to_broadcast([P, ST, P]),
                              gate_col[:, :].unsqueeze(2).to_broadcast([P, ST, P]), ALU.mult).then_inc(gate_ready, 1)
            dve.wait_ge(place_psum, 1)
            dve.wait_ge(iota_ready, 2)
            step(dve.tensor_scalar(over[:, :], ps[:, 5, ST * E:(ST + 1) * E], float(CAP), None, ALU.is_gt))
            step(dve.tensor_reduce(most[:, :], over[:, :], AX_X, ALU.add))
            dve.tensor_copy(more[:, :], most[:, :])
            earlier = cmp_gt[:, 0, :].rearrange("p (e j) -> p e j", j=E)
            low = lower[:, :].rearrange("p (e j) -> p e j", j=E)
            step(dve.tensor_tensor(earlier, low, over[:, :].unsqueeze(1).to_broadcast([P, E, E]), ALU.mult))
            step(dve.tensor_reduce(over_rank[:, :], earlier, AX_X, ALU.add))
            for m in range(MORE):
                ins = dve.scalar_tensor_tensor(out=over_hot[:, m, :], in0=over_rank[:, :], scalar=float(m),
                                               in1=over[:, :], op0=ALU.is_equal, op1=ALU.mult)
            step(ins)
            step(dve.tensor_tensor(scratch[:, 0, :, :], over_hot[:, :, :],
                                   slot_row[:, 0:E].unsqueeze(1).to_broadcast([P, MORE, E]), ALU.mult))
            step(dve.tensor_reduce(which32[:, :], scratch[:, 0, :, :], AX_X, ALU.add))
            step(dve.tensor_copy(which[:, :], which32[:, :]))
            step(dve.scalar_tensor_tensor(out=place[:, :, 0:E], in0=ps[:, 5, 0:ST * E].rearrange("p (t e) -> p t e", e=E),
                                          scalar=FAR, in1=taken[:, :, :], op0=ALU.subtract, op1=ALU.mult))
            step(dve.tensor_scalar(place[:, :, 0:E], place[:, :, 0:E], FAR, None, ALU.add))
            dve.sem_inc(more_ready, 1)
            step(dve.tensor_tensor(wn[:, :, 0:E], ex[:, :, 0:E], rinv[:, :].unsqueeze(2).to_broadcast([P, ST, E]),
                                   ALU.mult))
            for table in (place, wn):
                step(dve.tensor_tensor(scratch[:, :, :, :], table[:, :, 0:E].unsqueeze(2).to_broadcast([P, ST, MORE, E]),
                                       over_hot[:, :, :].unsqueeze(1).to_broadcast([P, ST, MORE, E]), ALU.mult))
                step(dve.tensor_reduce(table[:, :, E:NU], scratch[:, :, :, :], AX_X, ALU.add))
            step(dve.tensor_scalar(place[:, :, E:NU], place[:, :, E:NU], -float(CAP), None, ALU.add))
            step(dve.tensor_copy(ones_r[:, :], ones[:, :]))

            def picks(c):
                e, st = c // ST, c % ST
                return dve.tensor_scalar(pick[:, c, :], slot_row[:, :], place[:, st, e:e + 1], None, ALU.is_equal)

            def hidden(n, k, up_rows_, width, rows_, weight=None):
                p = k % 2
                dve.wait_ge(silu_done, n + 1)
                if weight is not None:
                    dve.wait_ge(u_psum, n + 1)
                dve.wait_ge(down_done, n + (1 - 2 + CREDIT))
                h = hid32[0:rows_, p, 0:width]
                dve.tensor_tensor(h, gated[0:rows_, p, 0:width], up_rows_, ALU.mult).then_inc(prod_done, 1)
                dve.wait_ge(prod_done, n + (1 + CREDIT))
                if weight is not None:
                    dve.wait_ge(wb_ready, 1)
                    step(dve.tensor_tensor(h, h, weight, ALU.mult))
                dve.tensor_copy(h_hi[0:rows_, p, 0:width], h).then_inc(hhi_ready, 1)
                dve.wait_ge(hhi_ready, n + 1)
                dve.tensor_tensor(h_lo[0:rows_, p, 0:width], h, h_hi[0:rows_, p, 0:width].bitcast(F32),
                                  ALU.subtract).then_inc(h_ready, 1)

            for n in range(SH):
                hidden(n, n, ps[:, 2 + n % 2, :], S, P, wb[:, :])
                for c in range(ST * n, ST * (n + 1)):
                    last_pick = picks(c)
                if n == 0:
                    dve.wait_ge(t_hi_ready, 1)
                    dve.tensor_tensor(t_lo[:, :, :], ln[:, :, :], t_hi[:, :, :].bitcast(F32),
                                      ALU.subtract).then_inc(t_lo_ready, 1)
            last_pick.then_inc(pick_ready, 1)
            dve.wait_ge(pick_ready, 1)

            def gathered(e, banks):
                dve.wait_ge(gather_lo_psum, e + 1)
                dve.tensor_copy(xg_lo[:, :, :].rearrange("p k c -> p (k c)"),
                                ps[:, banks + 2:banks + 4, :].rearrange("p a b -> p (a b)")).then_inc(xg_lo_ready, 1)

            def turned_places():
                dve.wait_ge(turned_psum, 1)
                dve.tensor_copy(places_t[0:NU, :], ps[0:NU, 4, :]).then_inc(turned_ready, 1)
                dve.wait_ge(turned_ready, 1)

            def own_row(e):
                dve.tensor_tensor(own_places[0:NU, :], places_t[0:NU, :],
                                  ident[0:NU, bass.ds(e, 1)].to_broadcast([NU, S]), ALU.mult).then_inc(own_ready, 1)

            def way_back(e):
                dve.wait_ge(place_b_psum, e + 1)
                for s in range(2):
                    ins = dve.tensor_scalar(back[:, s, :], ps[:, 4, :], slot_col[:, s:s + 1], None, ALU.is_equal)
                ins.then_inc(back_ready, 1)

            def low_output(e):
                dve.wait_ge(y_hi_ready, e + 1)
                dve.tensor_tensor(y_lo[:, :, :], ps[:, 2:4, :], y_hi[:, :, :].bitcast(F32),
                                  ALU.subtract).then_inc(y_lo_ready, 1)

            def add_output(e):
                for st in range(ST):
                    dve.wait_ge(scatter_psum, e * ST + (st + 1))
                    dve.wait_ge(added, e * ST + (st + 1))
                    weight = wn[:, st, bass.ds(e, 1)]
                    dve.scalar_tensor_tensor(out=x[:, st, :], in0=ps[:, 4 + st, :], scalar=weight, in1=x[:, st, :],
                                             op0=ALU.mult, op1=ALU.add).then_inc(added, 1)

            def unit(e, first=False, last=False):
                if not first:
                    way_back(e - 1)
                    low_output(e - 1)
                    own_row(e)
                for j in range(ET):
                    p, rows_ = (SH + j) % 2, HALF if j == ET - 1 else P
                    u = up_half[:, :] if j == ET - 1 else ps[:, p, CAP:2 * CAP]
                    hidden(e * ET + (SH + j), SH + j, u, CAP, rows_)
                    if j == 1:
                        if first:
                            turned_places()
                            own_row(e)
                        else:
                            add_output(e - 1)
                if last:
                    way_back(e)
                    low_output(e)
                    add_output(e)
                else:
                    gathered(e + 1, 4)

            dve.wait_ge(down_done, SH + CREDIT)
            for st in range(ST):
                dve.tensor_tensor(x[:, st, :], x[:, st, :], ps[:, 4 + st, :], ALU.add).then_inc(added, 1)
            gathered(0, 0)
            unit(0, first=True)
            final = dve.value_load(more[0:1, 0:1], min_val=0, max_val=MORE) + (E - 1)
            with dve.Fori(1, final) as e:
                unit(e)
            unit(final, last=True)


def kernel(x, ctx_1024, fside_BxSxS2_0, L0_xattn_Wq, L0_xattn_bq, L0_xattn_Wk, L0_xattn_bk, L0_xattn_Wv, L0_xattn_bv,
           L0_xattn_beta_risk, L0_xattn_beta_prio, L0_xattn_beta_impl, L0_attn_W_qkv, L0_attn_b_qkv, L0_ffn_gate_w,
           L0_ffn_experts_gate_up, L0_ffn_experts_down, L0_ffn_shared_gate_w, L0_ffn_shared_up_w,
           L0_ffn_shared_down_w, L0_ffn_shared_expert_gate_w):
    import numpy as np
    import concourse.bacc as bacc
    from concourse.bass_utils import run_bass_kernel_spmd

    def rows(w):
        w = np.asarray(w)
        return w.reshape(w.shape[0] // P, P, w.shape[1]).transpose(1, 0, 2)

    def columns(b):
        return np.asarray(b).reshape(-1, P).T

    ctx = np.asarray(ctx_1024)[0].reshape(CT, P, KC, P)
    fside = np.asarray(fside_BxSxS2_0)[0]
    stream1 = np.stack([ctx.transpose(0, 3, 2, 1).reshape(CT, P, D), fside.T.reshape(CT, P, S)], axis=2)

    gu = np.asarray(L0_ffn_experts_gate_up)
    dn = np.asarray(L0_ffn_experts_down).transpose(0, 2, 1)
    whole = (ET - 1) * P

    def turned(w, n=P):
        t = w.reshape(-1, n, KC, P)
        return t.transpose(0, 3, 2, 1).reshape(t.shape[0], P, KC * n)

    def tiles(gate_rows, up_rows, down_rows):
        return np.stack([turned(gate_rows), turned(up_rows), down_rows.reshape(-1, P, D)], axis=2)

    half_up = np.concatenate([gu[:, whole:NI], gu[:, NI + whole:]], axis=1)

    b_qkv = np.asarray(L0_attn_b_qkv)
    given = {
        "x_in": np.asarray(x)[0],
        "stream1": stream1,
        "ctx_in": ctx.reshape(CT // 2, 2, P, D).transpose(0, 2, 1, 3),
        "wq_in": rows(np.asarray(L0_xattn_Wq).T),
        "wk_in": rows(L0_xattn_Wk),
        "wv_in": rows(np.asarray(L0_xattn_Wv).T),
        "wqkv_in": rows(np.asarray(L0_attn_W_qkv).T),
        "gate_in": rows(np.concatenate([np.asarray(L0_ffn_gate_w), np.asarray(L0_ffn_shared_expert_gate_w)]).T),
        "shared_in": tiles(np.asarray(L0_ffn_shared_gate_w), np.asarray(L0_ffn_shared_up_w),
                           np.asarray(L0_ffn_shared_down_w).T),
        "full_in": tiles(gu[:, :whole], gu[:, NI:NI + whole], dn[:, :whole]),
        "half_up_in": turned(half_up),
        "half_down_in": dn[:, whole:],
        "cols_in": np.concatenate([columns(L0_xattn_bq), columns(L0_xattn_bk), columns(b_qkv[:2 * D])], axis=1),
        "bv_in": np.asarray(L0_xattn_bv).reshape(1, D),
        "bqkv_in": b_qkv[2 * D:].reshape(1, D),
        "betas_in": np.stack([np.asarray(L0_xattn_beta_risk), np.asarray(L0_xattn_beta_prio),
                              np.asarray(L0_xattn_beta_impl)]).reshape(1, 3),
    }
    given = {name: np.ascontiguousarray(a) for name, a in given.items()}
    nc = bacc.Bacc("TRN2", target_bir_lowering=False, num_devices=1)
    args = {name: nc.dram_tensor(name, a.shape, mybir.dt.from_np(a.dtype), kind="ExternalInput").ap()
            for name, a in given.items()}
    result = nc.dram_tensor("result", (S, D), F32, kind="ExternalOutput").ap()
    perceiver_layer(nc, out=result, **args)
    r = run_bass_kernel_spmd(nc, [given], core_ids=[0])
    return r.results[0]["result"].reshape(1, S, D)
```
